# Optimizing a Trainium2 kernel written in Bass

```python
import numpy as np
import jax
import jax.numpy as jnp

def _softmax(x, axis=-1):
    return jax.nn.softmax(x, axis=axis)

def _gelu(x):
    return jax.nn.gelu(x, approximate=True)

def _silu(x):
    return jax.nn.silu(x)

def _sigmoid(x):
    return jax.nn.sigmoid(x)

def _layernorm(x, axis=-1, eps=1e-05):
    m = jnp.mean(x, axis=axis, keepdims=True)
    v = jnp.var(x, axis=axis, keepdims=True)
    return (x - m) / jnp.sqrt(v + eps)

def _scatter_add(tgt, idx, src, axis=0):
    return tgt.at[idx].add(src)

def _segment_sum(src, seg, n):
    return jax.ops.segment_sum(src, seg, n)
kernel_name = 'mk_adaln_attn_ffn_d1_seqx_r2_e4ecda'

def setup_inputs(seed: int=0):
    np.random.seed(seed)
    _w = jnp.asarray

    def _rec_inputs():
        import jax
        import jax.numpy as jnp
        _rk = jax.random.key(seed)
        x = -0.000125 + 0.9999 * jax.random.normal(jax.random.fold_in(_rk, 1), (2, 2048, 512), jnp.float32)
        _lenS = 2048 - jax.random.randint(jax.random.fold_in(_rk, 7), (2,), 0, max(1, 2048 // 4) + 1, jnp.int32)
        _lenS2 = 2048 - jax.random.randint(jax.random.fold_in(_rk, 8), (2,), 0, max(1, 2048 // 4) + 1, jnp.int32)
        cond_1024 = 0.00513981 + 1.0024 * jax.random.normal(jax.random.fold_in(_rk, 11), (2, 512), jnp.float32)
        return (x, cond_1024)
    x, cond_1024 = _rec_inputs()

    def _L0_cond_setup():
        import jax, jax.numpy as jnp
        import numpy as np
        IN_FEATURES = 512
        OUT_FEATURES = 512
        BATCH = 32
        SEQ = 512
        EPS = 1e-08
        key = jax.random.key(seed)
        k1, k2, k3 = jax.random.split(key, 3)
        Efou = jax.random.normal(k1, (BATCH, SEQ, IN_FEATURES), dtype=jnp.float32)
        y = jax.random.normal(k2, (BATCH, IN_FEATURES), dtype=jnp.float32)
        weight = jax.random.normal(k3, (IN_FEATURES, OUT_FEATURES), dtype=jnp.float32)
        return {'Efou': Efou, 'y': y, 'weight': weight}
    _L0_cond_all = _L0_cond_setup()
    _L0_cond_in = {k: v for k, v in _L0_cond_all.items() if k in ('weight',)}
    del _L0_cond_all

    def _L0_attn_setup():
        import jax, jax.numpy as jnp
        import numpy as np
        D_MODEL = 512
        N_HEADS = 16
        D_HEAD = D_MODEL // N_HEADS
        WIN = 128
        NEG_INF = -1e+30

        def _band_mask(nb: int):
            ti = jnp.arange(WIN)[:, None]
            tj = jnp.arange(2 * WIN)[None, :]
            base = (tj >= ti + 1) & (tj <= ti + WIN)
            first = base & (tj >= WIN)
            rest = jnp.broadcast_to(base, (nb - 1, WIN, 2 * WIN))
            return jnp.concatenate([first[None], rest], axis=0)
        key = jax.random.key(seed)
        k1, k2, k3 = jax.random.split(key, 3)
        B, L = (4, 2048)
        x = jax.random.normal(k1, (B, L, D_MODEL), dtype=jnp.float32)
        w_qkv = jax.random.normal(k2, (D_MODEL, 3 * D_MODEL), dtype=jnp.float32) * (1.0 / np.sqrt(D_MODEL))
        w_out = jax.random.normal(k3, (D_MODEL, D_MODEL), dtype=jnp.float32) * (1.0 / np.sqrt(D_MODEL))
        return {'x': x, 'w_qkv': w_qkv, 'w_out': w_out}
    _L0_attn_all = _L0_attn_setup()
    _L0_attn_in = {k: v for k, v in _L0_attn_all.items() if k in ('w_qkv', 'w_out')}
    del _L0_attn_all

    def _L0_cond2_setup():
        import jax, jax.numpy as jnp
        import numpy as np
        N, T, D, H = (128, 256, 512, 512)
        key = jax.random.key(seed)
        k1, k2, k3, k4 = jax.random.split(key, 4)
        x = jax.random.normal(k1, (N, T, D), dtype=jnp.float32)
        h0 = jax.random.normal(k2, (N, H), dtype=jnp.float32)
        Wx = jax.random.normal(k3, (D, H), dtype=jnp.float32) / np.sqrt(D)
        Wh = jax.random.normal(k4, (H, H), dtype=jnp.float32) / np.sqrt(H)
        b = jnp.zeros((H,), dtype=jnp.float32)
        return {'x': x, 'h0': h0, 'Wx': Wx, 'Wh': Wh, 'b': b}
    _L0_cond2_all = _L0_cond2_setup()
    _L0_cond2_in = {k: v for k, v in _L0_cond2_all.items() if k in ('Wx', 'Wh', 'b')}
    del _L0_cond2_all

    def _L0_ffn_setup():
        import jax, jax.numpy as jnp
        import numpy as np
        HIDDEN = 512
        INTER = 2048
        key = jax.random.key(seed)
        k1, k2, k3, k4, k5 = jax.random.split(key, 5)
        hidden_states = jax.random.normal(k1, (4, 1024, HIDDEN), dtype=jnp.float32)
        W1 = jax.random.normal(k2, (HIDDEN, INTER), dtype=jnp.float32) * (1.0 / np.sqrt(HIDDEN))
        b1 = jax.random.normal(k3, (INTER,), dtype=jnp.float32) * 0.02
        W2 = jax.random.normal(k4, (INTER, HIDDEN), dtype=jnp.float32) * (1.0 / np.sqrt(INTER))
        b2 = jax.random.normal(k5, (HIDDEN,), dtype=jnp.float32) * 0.02
        return {'hidden_states': hidden_states, 'W1': W1, 'b1': b1, 'W2': W2, 'b2': b2}
    _L0_ffn_all = _L0_ffn_setup()
    _L0_ffn_in = {k: v for k, v in _L0_ffn_all.items() if k in ('W1', 'b1', 'W2', 'b2')}
    del _L0_ffn_all
    return {'x': x, 'cond_1024': cond_1024, 'L0_cond_weight': _L0_cond_in['weight'], 'L0_attn_w_qkv': _L0_attn_in['w_qkv'], 'L0_attn_w_out': _L0_attn_in['w_out'], 'L0_cond2_Wx': _L0_cond2_in['Wx'], 'L0_cond2_Wh': _L0_cond2_in['Wh'], 'L0_cond2_b': _L0_cond2_in['b'], 'L0_ffn_W1': _L0_ffn_in['W1'], 'L0_ffn_b1': _L0_ffn_in['b1'], 'L0_ffn_W2': _L0_ffn_in['W2'], 'L0_ffn_b2': _L0_ffn_in['b2']}

def reference(x, cond_1024, L0_cond_weight, L0_attn_w_qkv, L0_attn_w_out, L0_cond2_Wx, L0_cond2_Wh, L0_cond2_b, L0_ffn_W1, L0_ffn_b1, L0_ffn_W2, L0_ffn_b2):
    import jax
    import jax.numpy as jnp

    def _L0_cond_ref(Efou, y, weight):
        import jax, jax.numpy as jnp
        import numpy as np
        IN_FEATURES = 512
        OUT_FEATURES = 512
        BATCH = 32
        SEQ = 512
        EPS = 1e-08
        scale = 1.0 / np.sqrt(np.float32(weight.shape[0]))
        ys = y * scale
        d = jax.lax.rsqrt(jnp.einsum('bi,io->bo', ys * ys, weight * weight) + EPS)
        out = jnp.einsum('bsi,io->bso', Efou * ys[:, None, :], weight) * d[:, None, :]
        return out

    def _L0_attn_ref(x, w_qkv, w_out):
        import jax, jax.numpy as jnp
        import numpy as np
        D_MODEL = 512
        N_HEADS = 16
        D_HEAD = D_MODEL // N_HEADS
        WIN = 128
        NEG_INF = -1e+30

        def _band_mask(nb: int):
            ti = jnp.arange(WIN)[:, None]
            tj = jnp.arange(2 * WIN)[None, :]
            base = (tj >= ti + 1) & (tj <= ti + WIN)
            first = base & (tj >= WIN)
            rest = jnp.broadcast_to(base, (nb - 1, WIN, 2 * WIN))
            return jnp.concatenate([first[None], rest], axis=0)
        B, L, D = x.shape
        nb = L // WIN
        qkv = (x @ w_qkv).reshape(B, L, 3, N_HEADS, D_HEAD)
        q, k, v = (qkv[:, :, 0], qkv[:, :, 1], qkv[:, :, 2])

        def to_blocks(t):
            return t.transpose(0, 2, 1, 3).reshape(B, N_HEADS, nb, WIN, D_HEAD)
        qb, kb, vb = (to_blocks(q), to_blocks(k), to_blocks(v))
        zero_blk = jnp.zeros_like(kb[:, :, :1])
        k_kv = jnp.concatenate([jnp.concatenate([zero_blk, kb[:, :, :-1]], axis=2), kb], axis=3)
        v_kv = jnp.concatenate([jnp.concatenate([zero_blk, vb[:, :, :-1]], axis=2), vb], axis=3)
        scale = 1.0 / np.sqrt(D_HEAD)
        scores = jnp.einsum('bhnqd,bhnkd->bhnqk', qb, k_kv) * scale
        scores = jnp.where(_band_mask(nb), scores, NEG_INF)
        attn = jax.nn.softmax(scores, axis=-1)
        ob = jnp.einsum('bhnqk,bhnkd->bhnqd', attn, v_kv)
        out = ob.reshape(B, N_HEADS, L, D_HEAD).transpose(0, 2, 1, 3).reshape(B, L, D)
        return out @ w_out

    def _L0_cond2_ref(x, h0, Wx, Wh, b):
        import jax, jax.numpy as jnp
        import numpy as np
        N, T, D, H = (128, 256, 512, 512)
        xp = jnp.einsum('ntd,dh->nth', x, Wx) + b

        def step(prev_h, xp_t):
            next_h = jnp.tanh(xp_t + prev_h @ Wh)
            return (next_h, next_h)
        _, h = jax.lax.scan(step, h0, jnp.swapaxes(xp, 0, 1))
        return jnp.swapaxes(h, 0, 1)

    def _L0_ffn_ref(hidden_states, W1, b1, W2, b2):
        import jax, jax.numpy as jnp
        import numpy as np
        HIDDEN = 512
        INTER = 2048
        h = jax.nn.relu(jnp.einsum('bsh,hi->bsi', hidden_states, W1) + b1)
        return jnp.einsum('bsi,ih->bsh', h, W2) + b2
    x = x + _L0_attn_ref(_L0_cond_ref(x, cond_1024, L0_cond_weight), L0_attn_w_qkv, L0_attn_w_out)
    x = x + _L0_ffn_ref(_L0_cond2_ref(x, cond_1024, L0_cond2_Wx, L0_cond2_Wh, L0_cond2_b), L0_ffn_W1, L0_ffn_b1, L0_ffn_W2, L0_ffn_b2)
    return x

_drawn_inputs = setup_inputs


def setup_inputs(seed=0):
    import zlib

    import numpy as np

    out = dict(_drawn_inputs(seed))
    spreads = {'L0_cond2_b': (0.0, 0.1)}
    factors = {'L0_ffn_b1': 4.463, 'L0_ffn_b2': 3.248}
    for name, (base, spread) in spreads.items():
        noise = np.random.default_rng([zlib.crc32(name.encode()), seed]).standard_normal(out[name].shape)
        drawn = base * np.exp(spread * noise) if base else spread * noise
        out[name] = jnp.asarray(drawn.astype(out[name].dtype))
    for name, factor in factors.items():
        out[name] = (out[name] * factor).astype(out[name].dtype)
    return out
```

```python
from contextlib import ExitStack

import concourse.bass as bass
from concourse import mybir

P = 128
F32 = mybir.dt.float32
F32R = mybir.dt.float32r
I32 = mybir.dt.int32
ALU = mybir.AluOpType
ACT = mybir.ActivationFunctionType
AX_X = mybir.AxisListType.X
NEG_INF = -1e30
EPS = 1e-8
STATE_TOLERANCE = 2.0 ** -17
KB = 1024
SPLIT = ("xT", "x1T", "cT", "oT")
SBUF_FROM, SBUF_TO = 16512, 229344


class Item:

    def __init__(self, name):
        self.name, self.use, self.split = name, None, None
        self.kind, self.w = name.rstrip("_")[:-1], int(name.rstrip("_")[-1])


class Plan:

    def __init__(self, slots, first_use, first_half, first_split, use0=0, split0=0):
        self.slots, self.items = [[Item(name) for name in names] for names in slots], {}
        self.first_use, self.first_half, self.first_split = first_use, first_half, first_split
        self.begin = first_half + use0 // 2
        self.last = False
        use, split = use0, split0
        for row in self.slots:
            for item in row:
                self.items[item.name] = item
                if item.kind != "oT":
                    item.use, use = use, use + 1
                if item.kind in SPLIT:
                    item.split, split = split, split + 1


def block_kernel(nc, x, cond, w_cond, w_qkv, w_out, w_x, w_h, b_h, w1, b1, w2, b2, out):
    B, L, D = x.shape
    DC = D // P
    HEAD = 32
    GH = P // HEAD
    WIN = P
    TT = 2 * WIN
    BLK = TT // WIN
    NT = B * L // TT
    TPB = NT // B
    RUN = 32
    COLS = B * L // RUN
    CPB = COLS // B
    CPT = TT // RUN
    MAX_SWEEPS = CPB + 1
    F = w1.shape[1]
    FC = F // P
    TS = 4
    NF = RUN // TS
    HR = 4
    assert COLS == P and D == 512 and WIN == P and TPB % 2 == 0
    SCALE = float(HEAD) ** -0.5
    COND_SCALE = float(D) ** -0.5
    UNITS = BLK * DC

    x_tiles = x.rearrange("b l d -> (b l) d").rearrange("(n q p) d -> n p q d", q=BLK, p=P)
    out_by_run = out.rearrange("b l d -> (b l) d").rearrange("(p t) d -> p t d", t=RUN)
    residual = nc.dram_tensor("residual", (B * L, D), F32, kind="Internal").ap()
    res_tiles = residual.rearrange("(n q p) d -> n p q d", q=BLK, p=P)
    res_by_run = residual.rearrange("(p t) d -> p t d", t=RUN)
    xp_dram = nc.dram_tensor("xp_dram", (NT, P, DC * TT), F32, kind="Internal").ap()
    h_dram = nc.dram_tensor("h_dram", (RUN, P, DC * COLS), F32, kind="Internal").ap()

    def put(name, shape, at, dt=F32):
        n = 4
        for d in shape[1:]:
            n *= d
        assert SBUF_FROM + at + n <= SBUF_TO, (name, at + n)
        return nc.alloc_sbuf_tensor_at(name, shape, dt, offset=SBUF_FROM + at), at + n

    def pair(name, shape, at):
        hi, at = put(name + "_hi", shape, at, F32R)
        lo, at = put(name + "_lo", shape, at, F32R)
        return (hi, lo), at

    R1, R2 = 0, 64 * KB
    w_cond_s, a = pair("w_cond", [P, DC, D], R1)
    w_qkv_s, a = pair("w_qkv", [P, DC, 3 * D], a)
    assert a == R2
    w_out_s, a = pair("w_out", [P, DC, D], R2)
    w_x_s, a = pair("w_x", [P, DC, D], a)
    x_nat = [None, None]
    x_nat[0], a = put("x_nat0", [P, BLK, D], a)
    x_nat[1], a = put("x_nat1", [P, BLK, D], a)
    x1_nat, a = put("x1_nat", [P, BLK, D], a)
    xT, a = pair("xT", [P, DC, TT], a)
    cT_at = a
    cT, a = pair("cT", [P, DC, TT], a)
    kT, a = put("kT", [P, DC, 4, P], a)
    v_nat, a = put("v_nat", [P, 4, D], a)
    q_one = [None, None]
    q_one[0], a = put("q_one0", [P, GH, DC, TT], a)
    stage_at = a
    q_one[1], a = put("q_one1", [P, GH, DC, TT], a)
    own_T, prev_T, probs = [], [], []
    for group, name, n in ((own_T, "own_T", 2), (prev_T, "prev_T", 2), (probs, "probs", 4)):
        for i in range(n):
            t, a = put(f"{name}{i}", [P, GH, P], a)
            group.append(t)
    stage, _ = put("stage", [P, (a - stage_at) // 4], stage_at)
    oT, a = pair("oT", [P, DC, P], a)
    ident, a = put("ident", [P, P], a)
    own_mask, a = put("own_mask", [P, P], a)
    prev_mask, a = put("prev_mask", [P, P], a)
    xp_stage, a = put("xp_stage", [P, DC, TT], a)
    mix_end = a
    w_sq = (x1_nat, xp_stage)
    xp, _ = put("xp", [P, DC, COLS, RUN], R1)
    w1_hi_sb, a = put("w1_hi_sb", [P, DC, F], R2, F32R)
    states, a = put("states", [P, HR, DC, COLS], a)
    pre, a = put("pre", [P, 2, DC, COLS], a)
    starts, a = put("starts", [P, DC, COLS], a)
    drift, a = put("drift", [P, DC, COLS], a)
    w2_stage = [None] * FC
    for m in (FC - 2, FC - 1):
        w2_stage[m], a = put(f"w2_stage{m}", [P, D], a)
    assert a == cT_at
    w_h_sb, a = put("w_h_sb", [P, DC, D], a)
    w1_lo_sb, a = put("w1_lo_sb", [P, DC, F], a, F32R)
    w1_s = (w1_hi_sb, w1_lo_sb)
    w1_stage = [None, None]
    w1_stage[0], w1_stage_end = put("w1_stage0", [P, F], a)
    w1_stage[1], a = put("w1_stage1", [P, F], w1_stage_end)
    w2_stage_at = a
    for m in range(FC - 2):
        w2_stage[m], a = put(f"w2_stage{m}", [P, D], a)
    scan_end = a
    w2_s, a = pair("w2", [P, FC, D], R1)
    assert a == R2
    h_s, hid_s = [None, None], [None] * 4
    h_s[0], a = pair("h0", [P, TS, DC, COLS], R2 + 32 * KB)
    h_in_sb, a = put("h_in_sb", [P, TS, DC, COLS], w1_stage_end - 8 * KB)
    assert a == w1_stage_end
    a = cT_at
    for i in range(2):
        hid_s[i], a = pair(f"hid{i}", [P, TS * COLS], a)
    a = w1_stage_end
    for i in range(2, 4):
        hid_s[i], a = pair(f"hid{i}", [P, TS * COLS], a)
    assert a == w2_stage_at
    h_s[1], a = pair("h1", [P, TS, DC, COLS], a)
    res_in, a = put("res_in", [P, TS, D], a)
    y_out = [None, None]
    y_out[0], a = put("y_out0", [P, D], a)
    y_out[1], a = put("y_out1", [P, D], a)
    assert a <= scan_end
    a = max(mix_end, scan_end)
    hid_tmp = [None, None]
    hid_tmp[0], a = put("hid_tmp0", [P, TS * COLS], a)
    hid_tmp[1], a = put("hid_tmp1", [P, TS * COLS], a)
    b2_rows, a = put("b2_rows", [P, D], a)
    own_pred, a = put("own_pred", [P, P], a, I32)
    small = {}
    for name, shape in (("ones", [P, 1]), ("cond_T", [P, DC, B]), ("bh_T", [P, DC]), ("b1_T", [P, FC]),
                        ("ys", [P, DC, B]), ("ys_sq", [P, DC, B]), ("demod", [P, DC, B]), ("ys_tile", [P, NT, DC]),
                        ("demod_tile", [P, NT, DC]), ("before_tile", [P, NT // 2]), ("ys_now", [P, DC]),
                        ("demod_now", [P, DC]), ("before_now", [P, 1]), ("neg_max", [P, 4, GH]),
                        ("row_max", [P, 4, GH]), ("row_sum", [P, 4, GH]), ("row_inv", [P, 4, GH]),
                        ("worst", [P, 1]), ("off", [P, 1])):
        small[name], a = put(name, shape, (a + 31) // 32 * 32)
    (ones, cond_T, bh_T, b1_T, ys, ys_sq, demod, ys_tile, demod_tile, before_tile, ys_now, demod_now, before_now,
     neg_max, row_max, row_sum, row_inv, worst, off) = small.values()
    sweep_on, a = put("sweep_on", [1, 1], (a + 31) // 32 * 32, I32)

    with ExitStack() as ctx:
        def sem(name):
            return ctx.enter_context(nc.semaphore(name))

        ps = ctx.enter_context(nc.psum_tensor("ps", [P, 8, 512], F32))
        work_bank = [ps[:, 0, :], ps[:, 1, :]]
        score_bank = [ps[:, 2:4, :], ps[:, 4:6, :]]
        turn_bank = ps[:, 6, :].rearrange("p (r t) -> p r t", r=GH)
        o_bank = ps[:, 7, :].rearrange("p (g t) -> p g t", g=DC)

        w_in = [sem(f"w_in{i}") for i in range(6)]
        w_hi = sem("w_hi")
        w_lo = sem("w_lo")
        small_in = sem("small_in")
        setup_gps = sem("setup_gps")
        setup_dve = sem("setup_dve")
        setup_act = sem("setup_act")
        setup_pe = sem("setup_pe")
        x_in = [sem("x_in0"), sem("x_in1")]
        now_set = sem("now_set")
        work_full = sem("work_full")
        work_empty = [sem("work_empty0"), sem("work_empty1")]
        split_hi = sem("split_hi")
        scores_done = sem("scores_done")
        dve_step = sem("dve_step")
        select_gate = sem("select_gate")
        max_ready = sem("max_ready")
        exp_done = sem("exp_done")
        inv_ready = sem("inv_ready")
        norm_done = sem("norm_done")
        turn_done = sem("turn_done")
        masked = sem("masked")
        pv_done = sem("pv_done")
        o_ready = sem("o_ready")
        res_out = sem("res_out")
        xp_out = sem("xp_out")
        xp_in = sem("xp_in")
        w_h_in = sem("w_h_in")
        w1_in = [sem("w1_in0"), sem("w1_in1")]
        w1_hi = sem("w1_hi")
        w1_lo = sem("w1_lo")
        w2_in = sem("w2_in")
        w2_hi = sem("w2_hi")
        w2_lo = sem("w2_lo")
        mm_done = sem("mm_done")
        add_done = sem("add_done")
        h_done = sem("h_done")
        h_out = [sem(f"h_out{j}") for j in range(HR)]
        state_step = sem("state_step")
        off_ready = sem("off_ready")
        count_ready = sem("count_ready")
        flag_ready = sem("flag_ready")
        sp_gate = sem("sp_gate")
        scan_over = sem("scan_over")
        h_early = sem("h_early")
        h_in = sem("h_in")
        h_hi = sem("h_hi")
        h_lo = sem("h_lo")
        hid_full = sem("hid_full")
        relu_done = sem("relu_done")
        hid_hi = sem("hid_hi")
        hid_split = sem("hid_split")
        hid_used = sem("hid_used")
        y_full = sem("y_full")
        y_ready = sem("y_ready")
        res_back = sem("res_back")
        res_b2 = sem("res_b2")
        y_stored = [sem("y_stored0"), sem("y_stored1")]

        N_SMALL = 3 + B
        PART = DC * D
        parts = [(stage[:, 3 * PART:4 * PART], w_cond, w_cond_s, 0)]
        parts += [(stage[:, i * PART:(i + 1) * PART], w_qkv, w_qkv_s, i * D) for i in range(3)]
        parts += [(stage[:, 0:PART], w_out, w_out_s, 0), (stage[:, PART:2 * PART], w_x, w_x_s, 0)]
        parts = [(src.rearrange("p (c n) -> p c n", c=DC), w.rearrange("(c p) n -> p c n", p=P)[:, :, at:at + D],
                  [t[:, :, at:at + D] for t in dst]) for src, w, dst, at in parts]
        WEIGHTS = len(parts)
        LAG_T, LAG_V = 2, 3
        CREDIT = 4
        SLOTS = UNITS + LAG_V
        FL = 2
        H_AT = 12

        MID = [["x1T0", "x1T1"], ["xp0"], ["xp1"], ["xT0", "xT1"], ["cT0"], ["cT1"], ["q0"], ["oT0", "q1"],
               ["k0", "out0"], ["k1"], ["oT1", "v0", "v1", "out1"]]
        OWN_ONLY = ("oT", "out")
        TURNS = ("xT", "x1T")
        uses = sum(Item(n).kind != "oT" for s in MID for n in s)
        splits = sum(Item(n).kind in SPLIT for s in MID for n in s)
        before = Plan([["xT0", "xT1"], ["cT0", "cT1"], ["q0", "q1"], ["k0", "k1"], ["v0", "v1"]], 0, 0, 0)
        U0, S0 = len(before.items) - 4, 4 - 2
        assert uses % 2 == 0 and U0 % 2 == 0

        def plan_of(n, kind):
            counts = (n * uses + U0, n * (uses // 2) + U0 // 2, n * splits + S0)
            if kind == "first":
                return Plan([[] if s < 3 else MID[s] for s in range(SLOTS)], *counts, use0=4, split0=2)
            if kind == "last":
                plan = Plan([MID[s] if s < 3 else [i for i in MID[s] if Item(i).kind in OWN_ONLY] for s in range(SLOTS)]
                            + [["x1T0_", "x1T1_"], ["xp0_", "xp1_"]], *counts)
                plan.last = True
                return plan
            return Plan(MID, *counts)

        def steps_before(n, half):
            return n * 2 * UNITS + half * (DC + 1)

        def emptied(eng, plan, name):
            use = plan.items[name].use
            eng.wait_ge(work_empty[use % 2], 1 + plan.first_half + use // 2 + 1)

        def all_tiles(eng, tile):
            tile(0, 0, "first", 0)
            with eng.Fori(0, (NT - 2) // 2) as it:
                tile(it * 2 + 1, 1, "mid", it + 1)
                tile(it * 2 + 2, 0, "mid", it + 1)
            tile(NT - 1, 1, "last", NT // 2)

        def score_of(u, r):
            return score_bank[u % 2].rearrange("p b (h k) -> p (b h) k", h=2)[:, r, :]

        LAST = plan_of(NT - 1, "last")
        block = ctx.enter_context(nc.Block())

        @block.sync
        def _(sp):
            sp.sem_inc(res_out, 16)
            sp.sem_inc(xp_out, 16)
            for j in range(HR):
                sp.sem_inc(h_out[j], 16)
            for i in range(2):
                sp.sem_inc(y_stored[i], 16)
            sp.dma_start(x_nat[0][:, :, :], x_tiles[0]).then_inc(x_in[0], 16)
            for i in range(4):
                sp.dma_start(parts[i][0], parts[i][1]).then_inc(w_in[i], 16)
            sp.dma_start(x_nat[1][:, :, :], x_tiles[1]).then_inc(x_in[1], 16)
            for i in range(4, WEIGHTS):
                sp.wait_ge(w_lo, i - 2)
                sp.dma_start(parts[i][0], parts[i][1]).then_inc(w_in[i], 16)

            def store_xp(plan, name, n):
                emptied(sp, plan, name)
                sp.dma_start(xp_dram[bass.ds(n, 1)].rearrange("n p f -> (n p) f"),
                             xp_stage[:, :, :].rearrange("p c t -> p (c t)")).then_inc(xp_out, 16)

            def tile(n, par, kind, load):
                plan = plan_of(n, kind)
                if kind == "mid":
                    store_xp(plan, "xp1", n - 1)
                emptied(sp, plan, "out1")
                sp.dma_start(res_tiles[bass.ds(n, 1)].rearrange("n p q d -> (n p) q d"), x1_nat[:, :, :])\
                    .then_inc(res_out, 16)
                if load:
                    sp.dma_start(x_nat[par][:, :, :], x_tiles[bass.ds(n + 2, 1)].rearrange("n p q d -> (n p) q d"))\
                        .then_inc(x_in[par], 16)

            tile(0, 0, "first", True)
            with sp.Fori(0, (NT - 4) // 2) as it:
                tile(it * 2 + 1, 1, "mid", True)
                tile(it * 2 + 2, 0, "mid", True)
            tile(NT - 3, 1, "mid", True)
            tile(NT - 2, 0, "mid", False)
            mid = plan_of(NT - 2, "mid")
            sp.wait_ge(work_full, mid.first_use + mid.items["v1"].use + 1)

            def load_xp(n):
                sp.dma_start(xp[:, :, n * CPT:(n + 1) * CPT, :],
                             xp_dram[n].rearrange("p (c n t) -> p c n t", c=DC, t=RUN)).then_inc(xp_in, 16)

            sp.dma_start(w_h_sb[:, :, :], w_h.rearrange("(c p) n -> p c n", p=P)).then_inc(w_h_in, 16)
            sp.wait_ge(xp_out, 16 + 16 * (NT - 2))
            for n in range(NT - 2):
                load_xp(n)
            tile(NT - 1, 1, "last", False)
            sp.wait_ge(res_out, 16 + 16 * NT)

            def load_h(n, signal):
                sp.dma_start(h_in_sb[:, :, :, :].rearrange("p t c n -> p t (c n)"),
                             h_dram[bass.ds(n * TS, TS)].rearrange("t p f -> p t f")).then_inc(signal, 16)

            sp.wait_ge(flag_ready, 1)
            sweep, again = sp.alloc_register("sp_sweep"), sp.alloc_register("sp_again")
            sp.reg_mov(sweep, 0)
            sp.reg_mov(again, 1)
            with sp.While(lambda: sp.snap(again)):
                s = sp.snap(sweep, min_val=0, max_val=MAX_SWEEPS)

                def store_states(tr):
                    for j in range(HR):
                        t = tr * HR + j
                        sp.wait_ge(h_done, DC + (s * RUN + t + 1) * DC)
                        sp.dma_start(h_dram[bass.ds(t, 1)].rearrange("t p f -> (t p) f"),
                                     states[:, j, :, :].rearrange("p c n -> p (c n)")).then_inc(h_out[j], 16)

                EARLY = 5
                with sp.Fori(0, EARLY) as tr:
                    store_states(tr)
                sp.wait_ge(w1_lo, DC)
                for j in range(HR):
                    sp.wait_ge(h_out[j], 16 + (s * (RUN // HR) + EARLY - 1) * 16)
                load_h(0, h_early)
                with sp.Fori(EARLY, RUN // HR) as tr:
                    store_states(tr)
                sp.wait_ge(flag_ready, s + 2)
                sp.sem_inc(sp_gate, 1)
                sp.reg_add(sweep, sweep, 1)
                sp.reg_load(again, sweep_on[0:1, 0:1])

            sp.wait_ge(scan_over, 1)

            def ffn_tile(n, first, last):
                if first:
                    sp.wait_ge(w2_lo, FC)
                sp.wait_ge(y_ready, 1 + n * TS)
                sp.dma_start(res_in[:, :, :], res_by_run[:, bass.ds(n * TS, TS), :]).then_inc(res_back, 16)
                if not last:
                    sp.wait_ge(h_lo, n + 1)
                    load_h(n + 1, h_in)
                for q in range(TS):
                    sp.wait_ge(y_ready, 1 + n * TS + q + 1)
                    sp.dma_start(out_by_run[:, bass.ds(n * TS + q, 1), :].rearrange("p t d -> p (t d)"), y_out[q % 2][:, :])\
                        .then_inc(y_stored[q % 2], 16)

            ffn_tile(0, True, False)
            with sp.Fori(0, (NF - 2) // 2) as it:
                ffn_tile(it * 2 + 1, False, False)
                ffn_tile(it * 2 + 2, False, False)
            ffn_tile(NF - 1, False, True)
            for i in range(2):
                sp.wait_ge(y_stored[i], 16 + 16 * NF * TS // 2)

        @block.gpsimd
        def _(gp):
            nc.gpsimd.memset(ident[:, :], 0.0).then_inc(setup_gps, 1)
            nc.gpsimd.memset(own_mask[:, :], 1.0).then_inc(setup_gps, 1)
            nc.gpsimd.memset(prev_mask[:, :], 1.0).then_inc(setup_gps, 1)
            nc.gpsimd.memset(own_pred[:, :], 1).then_inc(setup_gps, 1)
            nc.gpsimd.memset(ones[:, :], 1.0).then_inc(setup_gps, 1)
            nc.gpsimd.memset(kT[:, :, 3, :], 0.0).then_inc(setup_gps, 1)
            nc.gpsimd.memset(v_nat[:, 3, :], 0.0).then_inc(setup_gps, 1)
            gp.wait_ge(setup_gps, 7)
            nc.gpsimd.affine_select(out=ident[:, :], in_=ident[:, :], compare_op=ALU.not_equal, fill=1.0,
                                    base=0, pattern=[[-1, P]], channel_multiplier=1).then_inc(setup_gps, 1)
            nc.gpsimd.affine_select(out=own_mask[:, :], in_=own_mask[:, :], compare_op=ALU.is_ge, fill=0.0,
                                    base=0, pattern=[[1, P]], channel_multiplier=-1).then_inc(setup_gps, 1)
            nc.gpsimd.affine_select(out=prev_mask[:, :], in_=prev_mask[:, :], compare_op=ALU.is_ge, fill=0.0,
                                    base=-1, pattern=[[-1, P]], channel_multiplier=1).then_inc(setup_gps, 1)
            nc.gpsimd.affine_select(out=own_pred[:, :], in_=own_pred[:, :], compare_op=ALU.is_ge, fill=0,
                                    base=0, pattern=[[-1, P]], channel_multiplier=1).then_inc(setup_gps, 1)
            nc.gpsimd.memset(q_one[0][:, :, :, :], 0.0).then_inc(setup_gps, 1)
            gp.wait_ge(w_lo, WEIGHTS)
            nc.gpsimd.memset(q_one[1][:, :, :, :], 0.0).then_inc(setup_gps, 1)

            def tile(n, par, kind, half):
                for u in range(UNITS):
                    gp.wait_ge(inv_ready, n * UNITS + u + 1)
                    nc.gpsimd.tensor_tensor(probs[u % 4][:, :, :], probs[u % 4][:, :, :],
                                            row_inv[:, u % 4, :].unsqueeze(2).to_broadcast([P, GH, P]),
                                            ALU.mult).then_inc(norm_done, 1)

            all_tiles(gp, tile)

            emptied(gp, LAST, "xp1_")
            gp.wait_ge(res_out, 16 + 16 * NT)
            gp.wait_ge(xp_out, 16 + 16 * (NT - 2))
            for k in range(2):
                gp.dma_start(w1_stage[k][:, :], w1[k * P:(k + 1) * P, :]).then_inc(w1_in[k], 16)
            for m in range(FC):
                gp.dma_start(w2_stage[m][:, :], w2[m * P:(m + 1) * P, :]).then_inc(w2_in, 16)
            for k in range(DC):
                gp.wait_ge(w1_in[k % 2], 16 * (k // 2 + 1))
                nc.gpsimd.tensor_copy(w1_s[0][:, k, :], w1_stage[k % 2][:, :]).then_inc(w1_hi, 1)
                gp.wait_ge(w1_hi, k + 1)
                nc.gpsimd.tensor_tensor(w1_s[1][:, k, :], w1_stage[k % 2][:, :], w1_s[0][:, k, :].bitcast(F32),
                                        ALU.subtract).then_inc(w1_lo, 1)
                if k + 2 < DC:
                    gp.wait_ge(w1_lo, k + 1)
                    gp.dma_start(w1_stage[k % 2][:, :], w1[(k + 2) * P:(k + 3) * P, :]).then_inc(w1_in[k % 2], 16)
            for m in range(FC):
                gp.wait_ge(w2_hi, m + 1)
                nc.gpsimd.tensor_tensor(w2_s[1][:, m, :], w2_stage[m][:, :], w2_s[0][:, m, :].bitcast(F32),
                                        ALU.subtract).then_inc(w2_lo, 1)
            with gp.Fori(0, NF) as n:
                gp.wait_ge(res_back, (n + 1) * 16)
                nc.gpsimd.tensor_tensor(res_in[:, :, :], res_in[:, :, :],
                                        b2_rows[:, :].unsqueeze(1).to_broadcast([P, TS, D]), ALU.add).then_inc(res_b2, 1)

        @block.scalar
        def _(act):
            for b in range(B):
                act.dma_start(cond_T[:, :, b], cond[b].rearrange("(c p) -> p c", p=P),
                              allow_slow_non_contiguous=True).then_inc(small_in, 16)
            act.dma_start(bh_T[:, :], b_h.rearrange("(c p) -> p c", p=P), allow_slow_non_contiguous=True).then_inc(small_in, 16)
            act.dma_start(b1_T[:, :], b1.rearrange("(c p) -> p c", p=P), allow_slow_non_contiguous=True).then_inc(small_in, 16)
            act.dma_start(b2_rows[:, :], b2.rearrange("(a n) -> a n", a=1).to_broadcast([P, D])).then_inc(small_in, 16)
            act.nop().then_inc(exp_done, CREDIT)
            act.nop().then_inc(h_done, DC)
            act.nop().then_inc(relu_done, 4)

            def w_part(i):
                act.wait_ge(w_in[i], 16)
                nc.scalar.activation(parts[i][2][0], parts[i][0], ACT.Copy).then_inc(w_hi, 1)

            w_part(0)
            act.wait_ge(setup_dve, 3)
            nc.scalar.activation(demod[:, :, :], ys[:, :, :], ACT.Sqrt).then_inc(setup_act, 1)

            def full(plan, item):
                act.wait_ge(work_full, plan.first_use + item.use + 1)

            def emit(plan, item, n, par):
                name, w = item.kind, item.w
                if name == "oT":
                    act.wait_ge(pv_done, CREDIT + n * UNITS + (w + 1) * DC)
                    nc.scalar.activation(oT[0][:, :, :], o_bank, ACT.Copy).then_inc(split_hi, 1)
                    return
                if name == "out":
                    return
                full(plan, item)
                bank = work_bank[item.use % 2]
                if name == "xT":
                    for j in range(2):
                        last = nc.scalar.activation(xT[0][:, 2 * w + j, :], bank[:, j * TT:(j + 1) * TT], ACT.Copy,
                                                    scale=ys_now[:, 2 * w + j:2 * w + j + 1])
                    last.then_inc(split_hi, 1)
                elif name == "cT":
                    for j in range(2):
                        last = nc.scalar.activation(cT[0][:, 2 * w + j, :], bank[:, j * TT:(j + 1) * TT], ACT.Copy,
                                                    scale=demod_now[:, 2 * w + j:2 * w + j + 1])
                    last.then_inc(split_hi, 1)
                elif name == "x1T":
                    nc.scalar.activation(xT[0][:, 2 * w:2 * w + 2, :], bank.rearrange("p (c t) -> p c t", c=2),
                                         ACT.Copy).then_inc(split_hi, 1)
                elif name == "q":
                    for r in range(GH):
                        rows = slice(r * HEAD, (r + 1) * HEAD)
                        last = nc.scalar.activation(q_one[par][rows, r, 2 * w:2 * w + 2, :],
                                                    bank[rows, :].rearrange("p (g t) -> p g t", g=2), ACT.Copy)
                    last.then_inc(work_empty[item.use % 2], 1)
                elif name == "k":
                    nc.scalar.activation(kT[:, 2 * w:2 * w + 2, 2 * par:2 * par + 2, :],
                                         bank.rearrange("p (g s t) -> p g s t", g=2, s=2), ACT.Copy)\
                        .then_inc(work_empty[item.use % 2], 1)
                elif name == "v":
                    nc.scalar.activation(v_nat[:, 2 * par + w, :], bank, ACT.Copy).then_inc(work_empty[item.use % 2], 1)
                elif name == "xp":
                    if w == 0 and not plan.last:
                        act.wait_ge(xp_out, 16 * n)
                    for j in range(2):
                        c = 2 * w + j
                        if plan.last:
                            k = NT - 1 if item.name[-1] == "_" else NT - 2
                            dst = xp[:, c, k * CPT:(k + 1) * CPT, :].rearrange("p n t -> p (n t)")
                        else:
                            dst = xp_stage[:, c, :]
                        last = nc.scalar.activation(dst, bank[:, j * TT:(j + 1) * TT], ACT.Identity,
                                                    bias=bh_T[:, c:c + 1])
                    last.then_inc(work_empty[item.use % 2], 1)

            act.wait_ge(now_set, 1)
            act.wait_ge(setup_gps, 12)
            for i, row in enumerate(before.slots):
                if 1 <= i < 4:
                    w_part(i)
                for item in row:
                    emit(before, item, 0, 0)
            w_part(4)
            w_part(5)

            def tile(n, par, kind, half):
                plan = plan_of(n, kind)
                for s in range(len(plan.slots)):
                    row = plan.slots[s]
                    if s == 3 and kind != "last":
                        act.wait_ge(now_set, n + 2)
                    if row and row[0].name[:2] == "oT":
                        emit(plan, row[0], n, par)
                        row = row[1:]
                    for item in row:
                        if item.kind in TURNS:
                            emit(plan, item, n, 1 - par)
                    if s < UNITS:
                        U = n * UNITS + s
                        act.wait_ge(max_ready, U + 1)
                        act.wait_ge(turn_done, CREDIT + U + 1 - 4)
                        for r in range(GH):
                            last = nc.scalar.activation(
                                probs[s % 4][:, r, :], score_of(s, r)[:, 0:P], ACT.Exp,
                                bias=neg_max[:, s % 4, r:r + 1], scale=SCALE, accum_out=row_sum[:, s % 4, r:r + 1])
                        last.then_inc(exp_done, 1)
                    for item in row:
                        if item.kind in TURNS:
                            continue
                        if kind == "first" and item.name == "q0":
                            act.wait_ge(setup_gps, 13)
                        emit(plan, item, n, 1 - par)

            all_tiles(act, tile)

            act.wait_ge(flag_ready, 1)
            sweep, again = act.alloc_register("act_sweep"), act.alloc_register("act_again")
            act.reg_mov(sweep, 0)
            act.reg_mov(again, 1)
            with act.While(lambda: act.snap(again)):
                s = act.snap(sweep, min_val=0, max_val=MAX_SWEEPS)
                with act.Fori(0, RUN // HR) as tr:
                    for j in range(HR):
                        G = s * RUN + tr * HR + j
                        act.wait_ge(h_out[j], 16 + (s * (RUN // HR) + tr) * 16)
                        for m in range(DC):
                            act.wait_ge(add_done, G * DC + m + 1)
                            nc.scalar.activation(states[:, j, m, :], pre[:, j % 2, m, :], ACT.Tanh).then_inc(h_done, 1)
                act.wait_ge(flag_ready, s + 2)
                act.reg_add(sweep, sweep, 1)
                act.reg_load(again, sweep_on[0:1, 0:1])

            act.wait_ge(scan_over, 1)

            def h_part(n, par, first=False):
                if not first:
                    act.wait_ge(h_in, n * 16)
                nc.scalar.activation(h_s[par][0][:, :, :, :].rearrange("p t c n -> p (t c n)"),
                                     h_in_sb[:, :, :, :].rearrange("p t c n -> p (t c n)"), ACT.Copy).then_inc(h_hi, 1)

            def ffn_tile(n, par, first, last):
                for m in range(FC):
                    if first and m < FC // 2:
                        if m == 0:
                            act.wait_ge(w2_in, 16 * FC)
                        for c in (2 * m, 2 * m + 1):
                            nc.scalar.activation(w2_s[0][:, c, :], w2_stage[c][:, :], ACT.Copy).then_inc(w2_hi, 1)
                    act.wait_ge(hid_full, n * FC + m + 1)
                    act.wait_ge(hid_split, 2 + n * FC + m - 1)
                    nc.scalar.activation(hid_tmp[m % 2][:, :], ps[:, m % 4, :], ACT.Relu, bias=b1_T[:, m:m + 1])\
                        .then_inc(relu_done, 1)
                    if m == H_AT and not last:
                        if first:
                            act.wait_ge(w2_lo, FC)
                        h_part(n + 1, 1 - par)

            h_part(0, 0, True)
            ffn_tile(0, 0, True, False)
            with act.Fori(0, (NF - 2) // 2) as it:
                ffn_tile(it * 2 + 1, 1, False, False)
                ffn_tile(it * 2 + 2, 0, False, False)
            ffn_tile(NF - 1, 1, False, True)

        @block.vector
        def _(dve):
            step = [0]

            def then(ins):
                step[0] += 1
                ins.then_inc(setup_dve, 1)
                dve.wait_ge(setup_dve, step[0])

            dve.sem_inc(masked, 1)
            dve.sem_inc(o_ready, 1)
            dve.sem_inc(y_ready, 1)
            dve.sem_inc(hid_split, 2)
            dve.wait_ge(small_in, 16 * N_SMALL)
            then(nc.vector.tensor_scalar(ys[:, :, :], cond_T[:, :, :], COND_SCALE, None, ALU.mult))
            for b in range(B):
                nc.vector.tensor_copy(ys_tile[:, b * TPB:(b + 1) * TPB, :],
                                      ys[:, :, b].unsqueeze(1).to_broadcast([P, TPB, DC]))
            nc.vector.memset(before_tile[:, :], 0.0)
            dve.wait_ge(w_in[0], 16)
            w_cond_st = stage[:, 3 * DC * D:4 * DC * D].rearrange("p (c n) -> p c n", c=DC)
            nc.vector.tensor_tensor(w_sq[0][:, :, :], w_cond_st[:, 0:2, :], w_cond_st[:, 0:2, :], ALU.mult)
            nc.vector.tensor_tensor(w_sq[1][:, :, :].rearrange("p c t -> p (c t)"),
                                    stage[:, 3 * DC * D + 2 * D:4 * DC * D], stage[:, 3 * DC * D + 2 * D:4 * DC * D], ALU.mult)
            then(nc.vector.tensor_tensor(ys_sq[:, :, :], ys[:, :, :], ys[:, :, :], ALU.mult))
            for b in range(B):
                i = b * TPB // 2
                nc.vector.memset(before_tile[:, i:i + 1], NEG_INF)

            def w_rest(i):
                dve.wait_ge(w_hi, i + 1)
                nc.vector.tensor_tensor(parts[i][2][1], parts[i][0], parts[i][2][0].bitcast(F32),
                                        ALU.subtract).then_inc(w_lo, 1)

            w_rest(0)
            dve.wait_ge(setup_pe, 1)
            then(nc.vector.tensor_scalar(ys[:, :, :], ps[:, 0, 0:DC * B].rearrange("p (c b) -> p c b", b=B),
                                         EPS, None, ALU.add))
            dve.wait_ge(setup_act, 1)
            then(nc.vector.reciprocal(demod[:, :, :], demod[:, :, :]))
            for b in range(B):
                last = nc.vector.tensor_copy(demod_tile[:, b * TPB:(b + 1) * TPB, :],
                                             demod[:, :, b].unsqueeze(1).to_broadcast([P, TPB, DC]))
            then(last)
            nc.vector.tensor_copy(ys_now[:, :], ys_tile[:, 0, :])
            nc.vector.tensor_copy(demod_now[:, :], demod_tile[:, 0, :]).then_inc(now_set, 1)
            dve.wait_ge(now_set, 1)
            dve.wait_ge(setup_gps, 12)

            def lo_part(plan, item, n, par):
                name, w = item.kind, item.w
                if name == "out":
                    dve.wait_ge(work_full, plan.first_use + item.use + 1)
                    if w == 0:
                        dve.wait_ge(res_out, 16 + n * 16)
                    nc.vector.tensor_tensor(x1_nat[:, w, :], work_bank[item.use % 2], x_nat[par][:, w, :], ALU.add)\
                        .then_inc(work_empty[item.use % 2], 1)
                    return
                if item.split is None:
                    return
                dve.wait_ge(split_hi, plan.first_split + item.split + 1)
                if name == "oT":
                    nc.vector.tensor_tensor(oT[1][:, :, :], o_bank, oT[0][:, :, :].bitcast(F32), ALU.subtract)\
                        .then_inc(o_ready, 1)
                    return
                bank = work_bank[item.use % 2]
                if name == "x1T":
                    last = nc.vector.tensor_tensor(xT[1][:, 2 * w:2 * w + 2, :], bank.rearrange("p (c t) -> p c t", c=2),
                                                   xT[0][:, 2 * w:2 * w + 2, :].bitcast(F32), ALU.subtract)
                else:
                    dst, factor = (xT, ys_now) if name == "xT" else (cT, demod_now)
                    for j in range(2):
                        c = 2 * w + j
                        last = nc.vector.scalar_tensor_tensor(
                            out=dst[1][:, c, :], in0=bank[:, j * TT:(j + 1) * TT], scalar=factor[:, c:c + 1],
                            in1=dst[0][:, c, :].bitcast(F32), op0=ALU.mult, op1=ALU.subtract)
                last.then_inc(work_empty[item.use % 2], 1)

            for i, row in enumerate(before.slots):
                if 1 <= i < 4:
                    w_rest(i)
                for item in row:
                    lo_part(before, item, 0, 0)
            w_rest(4)
            w_rest(5)

            def tile(n, par, kind, half):
                plan = plan_of(n, kind)
                count = [0]

                def own(ins):
                    count[0] += 1
                    ins.then_inc(dve_step, 1)
                    dve.wait_ge(dve_step, steps_before(n, half) + count[0])

                if par == 0:
                    own(nc.vector.tensor_copy(before_now[:, :], before_tile[:, bass.ds(half, 1)]))

                def max_of(u):
                    dve.wait_ge(scores_done, n * UNITS + u + 1)
                    s4 = score_bank[u % 2].rearrange("p b (h k) -> p (b h) k", h=2)
                    prev, own_s = s4[:, :, 0:P], s4[:, :, P:2 * P]
                    if par == 0 and u < DC:
                        own(nc.vector.tensor_scalar(prev, prev, before_now[:, 0:1], None, ALU.add))
                    dve.sem_inc(select_gate, 1)
                    own(nc.vector.copy_predicated(prev, own_pred[:, :].unsqueeze(1).to_broadcast([P, GH, P]), own_s))
                    own(nc.vector.reduce_max(row_max[:, u % 4, :], prev, AX_X))
                    nc.vector.tensor_scalar(neg_max[:, u % 4, :], row_max[:, u % 4, :], -SCALE, None, ALU.mult)\
                        .then_inc(max_ready, 1)

                def invert(u):
                    dve.wait_ge(exp_done, CREDIT + n * UNITS + u + 1)
                    nc.vector.reciprocal(row_inv[:, u % 4, :], row_sum[:, u % 4, :]).then_inc(inv_ready, 1)

                def mask(u):
                    dve.wait_ge(turn_done, CREDIT + n * UNITS + u + 1)
                    dve.wait_ge(pv_done, CREDIT + n * UNITS + u - 1)
                    nc.vector.tensor_tensor(own_T[u % 2][:, :, :], turn_bank,
                                            own_mask[:, :].unsqueeze(1).to_broadcast([P, GH, P]), ALU.mult)
                    nc.vector.tensor_tensor(prev_T[u % 2][:, :, :], turn_bank,
                                            prev_mask[:, :].unsqueeze(1).to_broadcast([P, GH, P]), ALU.mult)\
                        .then_inc(masked, 1)

                for s in range(len(plan.slots)):
                    row = plan.slots[s]
                    if s == 3 and kind != "last":
                        nc.vector.tensor_copy(ys_now[:, :], ys_tile[:, bass.ds(n + 1, 1), :].rearrange("p b c -> p (b c)"))
                        nc.vector.tensor_copy(demod_now[:, :], demod_tile[:, bass.ds(n + 1, 1), :].rearrange("p b c -> p (b c)"))\
                            .then_inc(now_set, 1)
                        dve.wait_ge(now_set, n + 2)
                    if row and row[0].name[:2] == "oT":
                        lo_part(plan, row[0], n, par)
                        row = row[1:]
                    if s < UNITS:
                        max_of(s)
                    for item in row:
                        if item.kind in TURNS:
                            lo_part(plan, item, n, par)
                    if 0 <= s - 1 < UNITS:
                        invert(s - 1)
                    if 0 <= s - LAG_T < UNITS:
                        mask(s - LAG_T)
                    for item in row:
                        if item.kind not in TURNS:
                            lo_part(plan, item, n, par)

            all_tiles(dve, tile)

            emptied(dve, LAST, "xp1_")
            dve.wait_ge(res_out, 16 + 16 * NT)
            dve.wait_ge(xp_out, 16 + 16 * (NT - 2))
            then(nc.vector.memset(starts[:, :, :], 0.0))
            for b in range(B):
                last = nc.vector.tensor_copy(starts[:, :, b * CPB:b * CPB + 1], cond_T[:, :, b:b + 1])
            then(last)
            nc.vector.tensor_copy(states[:, HR - 1, :, :], starts[:, :, :]).then_inc(flag_ready, 1)
            dve.wait_ge(xp_in, 16 * (NT - 2))

            sweep, again = dve.alloc_register("dve_sweep"), dve.alloc_register("dve_again")
            dve.reg_mov(sweep, 0)
            dve.reg_mov(again, 1)
            with dve.While(lambda: dve.snap(again)):
                s = dve.snap(sweep, min_val=0, max_val=MAX_SWEEPS)
                with dve.Fori(0, RUN // HR) as tr:
                    for j in range(HR):
                        G = s * RUN + tr * HR + j
                        for m in range(DC):
                            dve.wait_ge(mm_done, G * DC + m + 1)
                            nc.vector.tensor_tensor(
                                pre[:, j % 2, m, :], ps[:, (j % 2) * DC + m, 0:COLS],
                                xp[:, m, :, bass.ds(tr * HR + j, 1)].rearrange("p n t -> p (n t)"),
                                ALU.add).then_inc(add_done, 1)
                STEPS = B + 4
                ends = states[:, HR - 1, :, :]
                dve.wait_ge(h_done, DC + (s + 1) * RUN * DC)
                for b in range(B):
                    lo = b * CPB
                    nc.vector.tensor_tensor(drift[:, :, lo:lo + CPB - 1], ends[:, :, lo:lo + CPB - 1],
                                            starts[:, :, lo + 1:lo + CPB], ALU.subtract).then_inc(state_step, 1)
                dve.wait_ge(state_step, s * STEPS + B)
                for b in range(B):
                    lo = b * CPB
                    last = nc.vector.tensor_copy(starts[:, :, lo + 1:lo + CPB], ends[:, :, lo:lo + CPB - 1])
                by_b = drift[:, :, :].rearrange("p c (b n) -> p c b n", b=B)[:, :, :, 0:CPB - 1]
                nc.vector.tensor_tensor(by_b, by_b, by_b, ALU.mult).then_inc(state_step, 1)
                dve.wait_ge(state_step, s * STEPS + B + 1)
                nc.vector.tensor_reduce(worst[:, :], by_b, mybir.AxisListType.XYZ, ALU.max).then_inc(state_step, 1)
                dve.wait_ge(state_step, s * STEPS + B + 2)
                nc.vector.tensor_scalar(off[:, :], worst[:, :], STATE_TOLERANCE ** 2, None, ALU.is_gt)\
                    .then_inc(off_ready, 1)
                dve.wait_ge(h_early, (s + 1) * 16)
                for j in range(HR):
                    dve.wait_ge(h_out[j], 16 + (s + 1) * (RUN // HR) * 16)
                nc.vector.tensor_copy(ends, starts[:, :, :]).then_inc(state_step, 1)
                dve.wait_ge(state_step, s * STEPS + B + 3)
                dve.wait_ge(count_ready, s + 1)
                nc.vector.tensor_copy(sweep_on[0:1, 0:1], ps[0:1, 0, 0:1]).then_inc(flag_ready, 1)
                dve.nop().then_inc(state_step, 1)
                dve.wait_ge(flag_ready, s + 2)
                dve.reg_add(sweep, sweep, 1)
                dve.reg_load(again, sweep_on[0:1, 0:1])
            dve.nop().then_inc(scan_over, 1)

            def h_rest(n, par):
                dve.wait_ge(h_hi, n + 1)
                nc.vector.tensor_tensor(h_s[par][1][:, :, :, :].rearrange("p t c n -> p (t c n)"),
                                        h_in_sb[:, :, :, :].rearrange("p t c n -> p (t c n)"),
                                        h_s[par][0][:, :, :, :].rearrange("p t c n -> p (t c n)").bitcast(F32),
                                        ALU.subtract).then_inc(h_lo, 1)

            def ffn_tile(n, par, last):
                for m in range(FC):
                    dve.wait_ge(relu_done, 4 + n * FC + m + 1)
                    dve.wait_ge(hid_used, 4 + n * FC + m - 3)
                    nc.vector.tensor_copy(hid_s[m % 4][0][:, :], hid_tmp[m % 2][:, :]).then_inc(hid_hi, 1)
                    dve.wait_ge(hid_hi, n * FC + m + 1)
                    nc.vector.tensor_tensor(hid_s[m % 4][1][:, :], hid_tmp[m % 2][:, :], hid_s[m % 4][0][:, :].bitcast(F32),
                                            ALU.subtract).then_inc(hid_split, 1)
                    if m == H_AT and not last:
                        h_rest(n + 1, 1 - par)
                for q in range(TS):
                    dve.wait_ge(y_full, n * TS + q + 1)
                    dve.wait_ge(res_b2, n + 1)
                    dve.wait_ge(y_stored[q % 2], 16 + (n * (TS // 2) + q // 2) * 16)
                    nc.vector.tensor_tensor(y_out[q % 2][:, :], ps[:, 4 + q, :], res_in[:, q, :], ALU.add)\
                        .then_inc(y_ready, 1)

            h_rest(0, 0)
            ffn_tile(0, 0, False)
            with dve.Fori(0, (NF - 2) // 2) as it:
                ffn_tile(it * 2 + 1, 1, False)
                ffn_tile(it * 2 + 2, 0, False)
            ffn_tile(NF - 1, 1, True)

        @block.tensor
        def _(pe):
            for j in range(2):
                pe.nop().then_inc(work_empty[j], 1)
            pe.nop().then_inc(turn_done, CREDIT)
            pe.nop().then_inc(pv_done, CREDIT)
            pe.nop().then_inc(hid_used, 4)
            pe.wait_ge(setup_dve, 2)
            for m in range(DC):
                for k in range(DC):
                    sq = w_sq[k // 2][:, :, :].rearrange("p a b -> p (a b)")
                    at = (k % 2) * D + m * P
                    last = nc.tensor.matmul(ps[:, 0, m * B:(m + 1) * B], sq[:, at:at + P],
                                            ys_sq[:, k, :], start=(k == 0), stop=(k == DC - 1))
            last.then_inc(setup_pe, 1)
            pe.wait_ge(setup_dve, 3)
            pe.wait_ge(setup_gps, 12)

            def three(dst, a, b, first, last):
                nc.tensor.matmul(dst, a[0], b[0], start=first, stop=False)
                nc.tensor.matmul(dst, a[0], b[1], start=False, stop=False)
                return nc.tensor.matmul(dst, a[1], b[0], start=False, stop=last)

            def turn(bank, src, w):
                for j in range(2):
                    for q in range(BLK):
                        c = 2 * w + j
                        last = nc.tensor.transpose(bank[:, j * TT + q * P:j * TT + (q + 1) * P],
                                                   src[:, q, c * P:(c + 1) * P], ident[:, :])
                return last

            def product(bank, weight, col, src, w):
                for j in range(2):
                    c = col + (2 * w + j) * P
                    for k in range(DC):
                        last = three(bank[:, j * TT:(j + 1) * TT], [p[:, k, c:c + P] for p in weight],
                                     [p[:, k, :] for p in src], k == 0, k == DC - 1)
                return last

            def rows(bank, src, q, weight, col):
                for k in range(DC):
                    last = three(bank, [p[:, k, q * P:(q + 1) * P] for p in src],
                                 [p[:, k, col:col + D] for p in weight], k == 0, k == DC - 1)
                return last

            def emit(plan, item, par, half):
                name, w, bank = item.kind, item.w, work_bank[item.use % 2]
                pe.wait_ge(work_empty[item.use % 2], 1 + plan.first_half + item.use // 2)
                if name == "xT":
                    if w == 0:
                        pe.wait_ge(x_in[par], 16 * (half + 1))
                    last = turn(bank, x_nat[par], w)
                elif name == "cT":
                    if w == 0:
                        emptied(pe, plan, "xT1")
                    last = product(bank, w_cond_s, 0, xT, w)
                elif name == "q":
                    if w == 0:
                        emptied(pe, plan, "cT1")
                    last = product(bank, w_qkv_s, 0, cT, w)
                elif name == "k":
                    last = product(bank, w_qkv_s, D, cT, w)
                elif name == "v":
                    last = rows(bank, cT, w, w_qkv_s, 2 * D)
                elif name == "out":
                    last = rows(bank, oT, 0, w_out_s, 0)
                elif name == "x1T":
                    if w == 0 and item.name == "x1T0_":
                        emptied(pe, plan, "out1")
                    elif w == 0:
                        pe.wait_ge(work_empty[1], 1 + plan.begin)
                    last = turn(bank, x1_nat, w)
                elif name == "xp":
                    if w == 0:
                        emptied(pe, plan, item.name.replace("xp0", "x1T1"))
                    last = product(bank, w_x_s, 0, xT, w)
                last.then_inc(work_full, 1)

            for row in before.slots:
                for item in row:
                    if item.name == "cT0":
                        pe.wait_ge(w_lo, 1)
                    if item.name in ("q0", "k0", "v0"):
                        pe.wait_ge(w_lo, 2 + ("q0", "k0", "v0").index(item.name))
                    emit(before, item, 0, 0)

            def tile(n, par, kind, half):
                plan = plan_of(n, kind)

                def scores(u):
                    q, g = divmod(u, DC)
                    slot = 2 * par + q
                    if u == 0:
                        pe.wait_ge(work_empty[0], 1 + plan.begin)
                    pe.wait_ge(exp_done, CREDIT + n * UNITS + u - 1)
                    for r in range(GH):
                        for part, s in ((0, (slot - 1) % 4), (1, slot)):
                            last = nc.tensor.matmul(score_of(u, r)[:, part * P:(part + 1) * P],
                                                    q_one[par][:, r, g, q * P:(q + 1) * P], kT[:, g, s, :],
                                                    start=True, stop=True)
                    last.then_inc(scores_done, 1)

                def turn_probs(u):
                    pe.wait_ge(norm_done, n * UNITS + u + 1)
                    pe.wait_ge(masked, 1 + n * UNITS + u)
                    for r in range(GH):
                        last = nc.tensor.transpose(turn_bank[:, r, :], probs[u % 4][:, r, :], ident[:, :])
                    last.then_inc(turn_done, 1)

                def probs_v(u):
                    q, g = divmod(u, DC)
                    slot = 2 * par + q
                    if u == 0:
                        pe.wait_ge(work_empty[1], 1 + plan.begin)
                    pe.wait_ge(masked, 1 + n * UNITS + u + 1)
                    if g == 0:
                        pe.wait_ge(o_ready, 1 + n * BLK + q)
                    for probs_T, s, first in ((prev_T, (slot - 1) % 4, True), (own_T, slot, False)):
                        for r in range(GH):
                            cols = slice(g * P + r * HEAD, g * P + (r + 1) * HEAD)
                            last = nc.tensor.matmul(o_bank[r * HEAD:(r + 1) * HEAD, g, :], v_nat[:, s, cols],
                                                    probs_T[u % 2][:, r, :], start=first, stop=not first,
                                                    tile_position=(0, r * HEAD))
                    last.then_inc(pv_done, 1)

                for s in range(len(plan.slots)):
                    if s < UNITS:
                        scores(s)
                    for item in plan.slots[s]:
                        if item.kind in TURNS:
                            emit(plan, item, 1 - par, half)
                    if 0 <= s - LAG_T < UNITS:
                        turn_probs(s - LAG_T)
                    late = s - LAG_V == DC
                    if 0 <= s - LAG_V < UNITS and not late:
                        probs_v(s - LAG_V)
                    for item in plan.slots[s]:
                        if item.kind == "oT" or item.kind in TURNS:
                            continue
                        if item.kind == "out":
                            pe.wait_ge(o_ready, 1 + n * BLK + item.w + 1)
                            if kind == "first":
                                pe.wait_ge(w_lo, WEIGHTS)
                        emit(plan, item, 1 - par, half)
                    if late:
                        probs_v(s - LAG_V)

            all_tiles(pe, tile)

            pe.wait_ge(w_h_in, 16)
            pe.wait_ge(flag_ready, 1)
            sweep, again = pe.alloc_register("pe_sweep"), pe.alloc_register("pe_again")
            pe.reg_mov(sweep, 0)
            pe.reg_mov(again, 1)
            order = [(m, k) for m in (0, 1) for k in range(DC - 1)] + [(0, DC - 1), (1, DC - 1)] + \
                    [(m, k) for m in range(2, DC) for k in range(DC)]
            with pe.While(lambda: pe.snap(again)):
                s = pe.snap(sweep, min_val=0, max_val=MAX_SWEEPS)
                with pe.Fori(0, RUN // HR) as tr:
                    for j in range(HR):
                        G = s * RUN + tr * HR + j
                        waited = 0
                        for m, k in order:
                            if k >= waited:
                                pe.wait_ge(h_done, G * DC + k + 1)
                                waited = k + 1
                            ins = nc.tensor.matmul(ps[:, (j % 2) * DC + m, 0:COLS], w_h_sb[:, k, m * P:(m + 1) * P],
                                                   states[:, (j - 1) % HR, k, :], start=(k == 0), stop=(k == DC - 1))
                            if k == DC - 1:
                                ins.then_inc(mm_done, 1)
                pe.wait_ge(off_ready, s + 1)
                nc.tensor.matmul(ps[0:1, 0, 0:1], off[:, :], ones[:, :], start=True, stop=True).then_inc(count_ready, 1)
                pe.wait_ge(flag_ready, s + 2)
                pe.reg_add(sweep, sweep, 1)
                pe.reg_load(again, sweep_on[0:1, 0:1])

            pe.wait_ge(w1_lo, DC)

            def ffn_tile(n, par, first):
                for i in range(FC + FL):
                    if i < FC:
                        m = i
                        if m == 0:
                            pe.wait_ge(h_lo, n + 1)
                        pe.wait_ge(relu_done, n * FC + m + 1)
                        for k in range(DC):
                            ins = three(ps[:, m % 4, :].rearrange("p (t n) -> p t n", t=TS),
                                        [p[:, k, m * P:(m + 1) * P] for p in w1_s],
                                        [p[:, :, k, :] for p in h_s[par]], k == 0, k == DC - 1)
                        ins.then_inc(hid_full, 1)
                    if i >= FL:
                        m = i - FL
                        if m == 0:
                            pe.wait_ge(y_ready, 1 + n * TS)
                        if first:
                            pe.wait_ge(w2_lo, m + 1)
                        pe.wait_ge(hid_split, 2 + n * FC + m + 1)
                        for q in range(TS):
                            ins = three(ps[:, 4 + q, :], [p[:, q * P:(q + 1) * P] for p in hid_s[m % 4]],
                                        [p[:, m, :] for p in w2_s], m == 0, m == FC - 1)
                            if m == FC - 1:
                                ins.then_inc(y_full, 1)
                        if m < FC - 1:
                            ins.then_inc(hid_used, 1)
                        else:
                            pe.nop().then_inc(hid_used, 1)

            ffn_tile(0, 0, True)
            with pe.Fori(0, (NF - 2) // 2) as it:
                ffn_tile(it * 2 + 1, 1, False)
                ffn_tile(it * 2 + 2, 0, False)
            ffn_tile(NF - 1, 1, False)


_INS = ["x", "cond_1024", "L0_cond_weight", "L0_attn_w_qkv", "L0_attn_w_out", "L0_cond2_Wx", "L0_cond2_Wh",
        "L0_cond2_b", "L0_ffn_W1", "L0_ffn_b1", "L0_ffn_W2", "L0_ffn_b2"]


def kernel(**inputs):
    import numpy as _np
    import concourse.bacc as _bacc
    from concourse import mybir as _mybir
    from concourse.bass_utils import run_bass_kernel_spmd as _run

    nc = _bacc.Bacc("TRN2", target_bir_lowering=False, num_devices=1)
    arrays, args = {}, []
    for name in _INS:
        a = _np.ascontiguousarray(inputs[name])
        arrays[f"in_{name}_dram"] = a
        args.append(nc.dram_tensor(f"in_{name}_dram", a.shape, _mybir.dt.from_np(a.dtype), kind="ExternalInput").ap())
    out = nc.dram_tensor("out_dram", inputs["x"].shape, _mybir.dt.float32, kind="ExternalOutput").ap()
    block_kernel(nc, *args, out)
    r = _run(nc, [arrays], core_ids=[0])
    return r.results[0]["out_dram"]
```

```python
from contextlib import ExitStack

import concourse.bass as bass
from concourse import mybir

P = 128
F32 = mybir.dt.float32
F32R = mybir.dt.float32r
I32 = mybir.dt.int32
I8 = mybir.dt.int8
ALU = mybir.AluOpType
ACT = mybir.ActivationFunctionType
AX_X = mybir.AxisListType.X
NEG_INF = -1e30
EPS = 1e-8
STATE_TOLERANCE = 2.0 ** -17
KB = 1024
SPLIT = ("xT", "x1T", "cT", "q", "k", "oT")
SBUF_FROM, SBUF_TO = 16512, 229344


class Item:

    def __init__(self, name):
        self.name, self.use, self.split = name, None, None
        self.kind, self.w = name.rstrip("_")[:-1], int(name.rstrip("_")[-1])


class Plan:

    def __init__(self, slots, rounds, round_splits, use0, split0):
        self.slots, self.items = [[Item(name) for name in names] for names in slots], {}
        self.first_use, self.rounds, self.first_split, self.use0 = 2 * rounds, rounds, round_splits, use0
        self.last = False
        use, split = use0, split0
        for s, row in enumerate(self.slots):
            for item in row:
                self.items[item.name], item.slot = item, s
                if item.kind != "oT":
                    item.use, use = use, use + 1
                if item.kind in SPLIT:
                    item.split, split = split, split + 1
        self.uses, self.splits = use - use0, split - split0


def block_kernel(nc, x, cond, w_cond, w_qkv, w_out, w_x, w_h, b_h, w1, b1, w2, b2, out):
    B, L, D = x.shape
    DC = D // P
    HEAD = 32
    GH = P // HEAD
    WIN = P
    TT = 2 * WIN
    BLK = TT // WIN
    NT = B * L // TT
    TPB = NT // B
    RUN = 32
    COLS = B * L // RUN
    CPB = COLS // B
    CPT = TT // RUN
    MAX_SWEEPS = CPB + 1
    F = w1.shape[1]
    FC = F // P
    TS = 4
    NF = RUN // TS
    HR = 4
    assert TS == HR and COLS == P and D == 512 and WIN == P and TPB % 2 == 0
    SCALE = float(HEAD) ** -0.5
    COND_SCALE = float(D) ** -0.5
    UNITS = BLK * DC

    x_tiles = x.rearrange("b l d -> (b l) d").rearrange("(n q p) d -> n p q d", q=BLK, p=P)
    out_by_run = out.rearrange("b l d -> (b l) d").rearrange("(p t) d -> p t d", t=RUN)
    residual = nc.dram_tensor("residual", (B * L, D), F32, kind="Internal").ap()
    res_tiles = residual.rearrange("(n q p) d -> n p q d", q=BLK, p=P)
    res_by_run = residual.rearrange("(p t) d -> p t d", t=RUN)
    xp_dram = nc.dram_tensor("xp_dram", (NT, P, DC * TT), F32, kind="Internal").ap()
    h_dram = nc.dram_tensor("h_dram", (RUN, P, DC * COLS), F32, kind="Internal").ap()

    def put(name, shape, at, dt=F32):
        n = 4
        for d in shape[1:]:
            n *= d
        assert SBUF_FROM + at + n <= SBUF_TO, (name, at + n)
        return nc.alloc_sbuf_tensor_at(name, shape, dt, offset=SBUF_FROM + at), at + n

    def pair(name, shape, at):
        hi, at = put(name + "_hi", shape, at, F32R)
        lo, at = put(name + "_lo", shape, at, F32R)
        return (hi, lo), at

    R1, R2 = 0, 64 * KB
    w_cond_s, a = pair("w_cond", [P, DC, D], R1)
    w_qkv_s, a = pair("w_qkv", [P, DC, 3 * D], a)
    assert a == R2
    w_out_s, a = pair("w_out", [P, DC, D], R2)
    w_x_s, a = pair("w_x", [P, DC, D], a)
    x_nat = [None, None]
    x_nat[0], a = put("x_nat0", [P, BLK, D], a)
    x_nat[1], a = put("x_nat1", [P, BLK, D], a)
    x1_nat, a = put("x1_nat", [P, BLK, D], a)
    x1T_at = a
    x1T, a = pair("x1T", [P, DC, TT], a)
    cT_at = a
    cT, a = pair("cT", [P, DC, TT], a)
    kT, a = pair("kT", [P, DC, 4, P], a)
    v_nat, a = put("v_nat", [P, 4, D], a)
    qT, a = pair("qT", [P, DC, TT], a)
    xT, a = pair("xT", [P, DC, TT], a)
    own_at = a
    own_T, prev_T, probs = [], [], []
    for group, name, n in ((own_T, "own_T", 2), (prev_T, "prev_T", 2), (probs, "probs", 4)):
        if group is probs:
            probs_at = a
        for i in range(n):
            t, a = put(f"{name}{i}", [P, GH, P], a)
            group.append(t)
    oT, a = pair("oT", [P, DC, P], a)
    ident, a = put("ident", [P, P], a)
    own_mask, a = put("own_mask", [P, P], a)
    prev_mask, a = put("prev_mask", [P, P], a)
    xp_stage, a = put("xp_stage", [P, DC, TT], a)
    stage_v, a = put("stage_v", [P, DC, D], a)
    stage_own, stage_probs, stage_q = (put(name, [P, DC, D], at)[0] for name, at in (
        ("stage_own", own_at), ("stage_probs", probs_at), ("stage_q", x1T_at)))
    mix_end = a
    w_sq = (x1_nat, xp_stage)
    xp, _ = put("xp", [P, DC, COLS, RUN], R1)
    w1_hi_sb, a = put("w1_hi_sb", [P, DC, F], R2, F32R)
    states, a = put("states", [P, HR, DC, COLS], a)
    starts, a = put("starts", [P, DC, COLS], a)
    drift, a = put("drift", [P, DC, COLS], a)
    assert a == x1T_at
    pre, a = put("pre", [P, 2, DC, COLS], a)
    w2_stage = [None] * FC
    for m in (FC - 2, FC - 1):
        w2_stage[m], a = put(f"w2_stage{m}", [P, D], a)
    assert a == cT_at
    w_h_sb, a = put("w_h_sb", [P, DC, D], a)
    w1_lo_sb, a = put("w1_lo_sb", [P, DC, F], a, F32R)
    w1_s = (w1_hi_sb, w1_lo_sb)
    w1_stage = [None, None]
    w1_stage[0], w1_stage_end = put("w1_stage0", [P, F], a)
    w1_stage[1], a = put("w1_stage1", [P, F], w1_stage_end)
    w2_stage_at = a
    for m in range(FC - 2):
        w2_stage[m], a = put(f"w2_stage{m}", [P, D], a)
    scan_end = a
    w2_s, a = pair("w2", [P, FC, D], R1)
    assert a == R2
    h_s, hid_s = [None, None], [None] * 4
    h_first, _ = put("h_first", [P, TS, DC, COLS], w1_stage_end - 8 * KB)
    h0_lo, _ = put("h0_lo", [P, TS, DC, COLS], w1_stage_end - 8 * KB, F32R)
    h0_hi, a = put("h0_hi", [P, TS, DC, COLS], w1_stage_end, F32R)
    h_s[0] = (h0_hi, h0_lo)
    assert a == w2_stage_at
    h_s[1], a = pair("h1", [P, TS, DC, COLS], a)
    res_in, a = put("res_in", [P, TS, D], a)
    y_out = [None, None]
    y_out[0], a = put("y_out0", [P, D], a)
    y_out[1], a = put("y_out1", [P, D], a)
    assert a <= scan_end
    a = cT_at
    for i in range(2):
        hid_s[i], a = pair(f"hid{i}", [P, TS * COLS], a)
    h_in_sb, a = put("h_in_sb", [P, TS, DC, COLS], R2 + 32 * KB)
    for i in range(2, 4):
        hid_s[i], a = pair(f"hid{i}", [P, TS * COLS], a)
    assert a <= cT_at
    a = scan_end
    hid_tmp = [None, None]
    hid_tmp[0], a = put("hid_tmp0", [P, TS * COLS], a)
    hid_tmp[1], a = put("hid_tmp1", [P, TS * COLS], a)
    b2_rows, a = put("b2_rows", [P, D], a)
    a = max(mix_end, a)
    own_pred, a = put("own_pred", [P, P], a, I8)
    small = {}
    for name, shape in (("ones", [P, 1]), ("cond_T", [P, DC, B]), ("bh_T", [P, DC]), ("b1_T", [P, FC]),
                        ("ys", [P, DC, B]), ("ys_sq", [P, DC, B]), ("demod", [P, DC, B]), ("ys_tile", [P, NT, DC]),
                        ("demod_tile", [P, NT, DC]), ("before_tile", [P, NT // 2]), ("ys_now", [P, DC]),
                        ("demod_now", [P, DC]), ("before_now", [P, 1]), ("neg_max", [P, 4, GH]),
                        ("row_max", [P, 4, GH]), ("row_sum", [P, 4, GH]), ("row_inv", [P, 4, GH]),
                        ("worst", [P, 1]), ("off", [P, 1])):
        small[name], a = put(name, shape, (a + 31) // 32 * 32)
    (ones, cond_T, bh_T, b1_T, ys, ys_sq, demod, ys_tile, demod_tile, before_tile, ys_now, demod_now, before_now,
     neg_max, row_max, row_sum, row_inv, worst, off) = small.values()
    sweep_on, a = put("sweep_on", [1, 1], (a + 31) // 32 * 32, I32)

    with ExitStack() as ctx:
        def sem(name):
            return ctx.enter_context(nc.semaphore(name))

        ps = ctx.enter_context(nc.psum_tensor("ps", [P, 8, 512], F32))
        work_bank = [ps[:, 0, :], ps[:, 1, :]]
        score_bank = [ps[:, 2:4, :], ps[:, 4:6, :]]
        turn_bank = ps[:, 6, :].rearrange("p (r t) -> p r t", r=GH)
        o_bank = ps[:, 7, :].rearrange("p (g t) -> p g t", g=DC)

        w_in = [sem(f"w_in{i}") for i in range(6)]
        w_hi = sem("w_hi")
        w_lo = sem("w_lo")
        cond_in = sem("cond_in")
        biases_in = sem("biases_in")
        b2_in = sem("b2_in")
        setup_gps = sem("setup_gps")
        setup_dve = sem("setup_dve")
        setup_act = sem("setup_act")
        setup_pe = sem("setup_pe")
        x_in = [sem("x_in0"), sem("x_in1")]
        now_set = sem("now_set")
        demod_set = sem("demod_set")
        work_full = sem("work_full")
        work_empty = [sem("work_empty0"), sem("work_empty1")]
        split_hi = sem("split_hi")
        scores_done = sem("scores_done")
        dve_step = sem("dve_step")
        select_gate = sem("select_gate")
        max_ready = sem("max_ready")
        exp_done = sem("exp_done")
        inv_ready = sem("inv_ready")
        norm_done = sem("norm_done")
        turn_done = sem("turn_done")
        masked = sem("masked")
        pv_done = sem("pv_done")
        o_ready = sem("o_ready")
        res_out = sem("res_out")
        xp_out = sem("xp_out")
        xp_in = sem("xp_in")
        w_h_in = sem("w_h_in")
        w1_in = [sem("w1_in0"), sem("w1_in1")]
        w1_hi = sem("w1_hi")
        w1_lo = sem("w1_lo")
        w2_in = sem("w2_in")
        w2_hi = sem("w2_hi")
        w2_lo = sem("w2_lo")
        mm_done = sem("mm_done")
        add_done = sem("add_done")
        h_done = sem("h_done")
        h_out = [sem(f"h_out{j}") for j in range(HR)]
        state_step = sem("state_step")
        off_ready = sem("off_ready")
        count_ready = sem("count_ready")
        flag_ready = sem("flag_ready")
        sp_gate = sem("sp_gate")
        scan_over = sem("scan_over")
        h_early = sem("h_early")
        h_in = sem("h_in")
        h_first_hi = sem("h_first_hi")
        h_hi = sem("h_hi")
        h_lo = sem("h_lo")
        hid_full = sem("hid_full")
        relu_done = sem("relu_done")
        hid_hi = sem("hid_hi")
        hid_split = sem("hid_split")
        hid_used = sem("hid_used")
        y_full = sem("y_full")
        y_ready = sem("y_ready")
        res_back = sem("res_back")
        res_b2 = sem("res_b2")
        y_stored = [sem("y_stored0"), sem("y_stored1")]

        SET_IDENT, SET_ALL = 10, 12
        parts = [(stage_probs, w_cond, w_cond_s, 0), (stage_own, w_qkv, w_qkv_s, D), (stage_q, w_qkv, w_qkv_s, 0),
                 (stage_v, w_qkv, w_qkv_s, 2 * D), (stage_probs, w_out, w_out_s, 0), (stage_own, w_x, w_x_s, 0)]
        parts = [(src[:, :, :], w.rearrange("(c p) n -> p c n", p=P)[:, :, at:at + D],
                  [t[:, :, at:at + D] for t in dst]) for src, w, dst, at in parts]
        by_unit = w_out.rearrange("(r g d) n -> r d g n", g=DC, d=HEAD)
        STAGED_AFTER = {4: 1, 5: 2}
        WEIGHTS = len(parts)
        LAG_T, LAG_V = 4, 5
        CREDIT = 4
        SLOTS = UNITS + LAG_V
        FL = 2
        H_AT = 12

        MID = [["v1_", "x1T0", "x1T1"], [], ["xp0", "xT0"], ["xp1", "xT1"], ["cT0"], ["cT1"], ["k0"], ["k1"],
               ["oT0", "q0"], [], ["q1"], ["out0"], ["oT1", "v0", "out1"]]
        FIRST = [["xT0", "xT1"], ["cT0"], ["cT1"], [], ["k0"], ["k1"], [], [],
                 ["oT0", "q0"], ["q1"], [], ["out0"], ["oT1", "v0", "out1"]]
        ENDING = [["v1_", "x1T0", "x1T1"], [], ["xp0"], [], [], ["xp1"], [], [],
                  ["oT0"], ["out0"], [], [], ["oT1", "out1"], ["x1T0_", "x1T1_"], ["xp0_", "xp1_"]]
        BEFORE = [["xT0", "xT1"], ["cT0", "cT1"], ["k0", "k1"], ["q0", "q1"], ["v0", "v1"]]
        HALF_AHEAD = ("q1",)
        TURNS = ("xT", "x1T")
        before = Plan(BEFORE, 0, 0, 0, 0)
        first = Plan(FIRST, 0, 0, before.uses, before.splits)
        mid = Plan(MID, 0, 0, 0, 0)
        USE0 = before.uses + first.uses - mid.uses
        SPLIT0 = before.splits + first.splits - mid.splits
        assert mid.uses % 2 == 0 and len(MID) == len(FIRST) == SLOTS

        def plan_of(n, kind):
            if kind == "first":
                return first
            plan = Plan(ENDING if kind == "last" else MID, n * (mid.uses // 2), n * mid.splits, USE0, SPLIT0)
            plan.last = kind == "last"
            return plan

        def steps_before(n, half):
            return n * 2 * UNITS + half * (DC + 1)

        def emptied(eng, plan, name):
            use = plan.items[name].use
            eng.wait_ge(work_empty[use % 2], 1 + plan.rounds + use // 2 + 1)

        def last_emptied(eng, plan):
            use = plan.use0 - 1
            eng.wait_ge(work_empty[use % 2], 1 + plan.rounds + use // 2 + 1)

        def all_tiles(eng, tile):
            tile(0, 0, "first", 0)
            with eng.Fori(0, (NT - 2) // 2) as it:
                tile(it * 2 + 1, 1, "mid", it + 1)
                tile(it * 2 + 2, 0, "mid", it + 1)
            tile(NT - 1, 1, "last", NT // 2)

        def scores_of(par, u):
            all_s = score_bank[u % 2].rearrange("p b (h k) -> p (b h) k", h=2)
            first, second = all_s[:, :, 0:P], all_s[:, :, P:2 * P]
            return (all_s, second, first) if par == 0 and u < DC else (all_s, first, second)

        LAST = plan_of(NT - 1, "last")
        block = ctx.enter_context(nc.Block())

        @block.sync
        def _(sp):
            sp.sem_inc(res_out, 16)
            sp.sem_inc(xp_out, 16)
            for j in range(HR):
                sp.sem_inc(h_out[j], 16)
            for i in range(2):
                sp.sem_inc(y_stored[i], 16)
            sp.dma_start(x_nat[0][:, :, :], x_tiles[0]).then_inc(x_in[0], 16)
            for i in range(4):
                sp.dma_start(parts[i][0], parts[i][1]).then_inc(w_in[i], 16)
            sp.dma_start(x_nat[1][:, :, :], x_tiles[1]).then_inc(x_in[1], 16)
            for i in range(4, WEIGHTS):
                sp.wait_ge(w_lo, STAGED_AFTER[i])
                if i == 4:
                    for r in range(GH):
                        sp.dma_start(stage_probs[r * HEAD:(r + 1) * HEAD, :, :], by_unit[r]).then_inc(w_in[i], 16)
                else:
                    sp.dma_start(parts[i][0], parts[i][1]).then_inc(w_in[i], 16)

            def store_xp(plan, name, n):
                emptied(sp, plan, name)
                sp.dma_start(xp_dram[bass.ds(n, 1)].rearrange("n p f -> (n p) f"),
                             xp_stage[:, :, :].rearrange("p c t -> p (c t)")).then_inc(xp_out, 16)

            def tile(n, par, kind, load):
                plan = plan_of(n, kind)
                if kind == "mid":
                    store_xp(plan, "xp1", n - 1)
                emptied(sp, plan, "out1")
                sp.dma_start(res_tiles[bass.ds(n, 1)].rearrange("n p q d -> (n p) q d"), x1_nat[:, :, :])\
                    .then_inc(res_out, 16)
                if load:
                    sp.dma_start(x_nat[par][:, :, :], x_tiles[bass.ds(n + 2, 1)].rearrange("n p q d -> (n p) q d"))\
                        .then_inc(x_in[par], 16)

            tile(0, 0, "first", True)
            with sp.Fori(0, (NT - 4) // 2) as it:
                tile(it * 2 + 1, 1, "mid", True)
                tile(it * 2 + 2, 0, "mid", True)
            tile(NT - 3, 1, "mid", True)
            tile(NT - 2, 0, "mid", False)
            sp.wait_ge(work_full, LAST.first_use + LAST.items["v1_"].use + 1)

            def load_xp(n):
                sp.dma_start(xp[:, :, n * CPT:(n + 1) * CPT, :],
                             xp_dram[n].rearrange("p (c n t) -> p c n t", c=DC, t=RUN)).then_inc(xp_in, 16)

            sp.dma_start(w_h_sb[:, :, :], w_h.rearrange("(c p) n -> p c n", p=P)).then_inc(w_h_in, 16)
            sp.wait_ge(xp_out, 16 + 16 * (NT - 2))
            for n in range(NT - 2):
                load_xp(n)
            tile(NT - 1, 1, "last", False)
            sp.wait_ge(res_out, 16 + 16 * NT)

            def load_h(n, to, signal):
                sp.dma_start(to[:, :, :, :].rearrange("p t c n -> p t (c n)"),
                             h_dram[bass.ds(n * TS, TS)].rearrange("t p f -> p t f")).then_inc(signal, 16)

            sp.wait_ge(flag_ready, 1)
            sweep, again = sp.alloc_register("sp_sweep"), sp.alloc_register("sp_again")
            sp.reg_mov(sweep, 0)
            sp.reg_mov(again, 1)
            with sp.While(lambda: sp.snap(again)):
                s = sp.snap(sweep, min_val=0, max_val=MAX_SWEEPS)

                def store_states(tr):
                    for j in range(HR):
                        t = tr * HR + j
                        sp.wait_ge(h_done, DC + (s * RUN + t + 1) * DC)
                        sp.dma_start(h_dram[bass.ds(t, 1)].rearrange("t p f -> (t p) f"),
                                     states[:, j, :, :].rearrange("p c n -> p (c n)")).then_inc(h_out[j], 16)

                EARLY = 5
                with sp.Fori(0, EARLY) as tr:
                    store_states(tr)
                sp.wait_ge(w1_lo, DC)
                for j in range(HR):
                    sp.wait_ge(h_out[j], 16 + (s * (RUN // HR) + EARLY - 1) * 16)
                load_h(0, h_first, h_early)
                with sp.Fori(EARLY, RUN // HR) as tr:
                    store_states(tr)
                sp.wait_ge(flag_ready, s + 2)
                for j in range(HR):
                    sp.wait_ge(h_out[j], 16 + (s + 1) * (RUN // HR) * 16)
                sp.sem_inc(sp_gate, 1)
                sp.reg_add(sweep, sweep, 1)
                sp.reg_load(again, sweep_on[0:1, 0:1])

            sp.wait_ge(scan_over, 1)

            def ffn_tile(n, first, last):
                if first:
                    sp.wait_ge(w2_lo, FC)
                sp.wait_ge(y_ready, 1 + n * TS)
                sp.dma_start(res_in[:, :, :], res_by_run[:, bass.ds(n * TS, TS), :]).then_inc(res_back, 16)
                if not last:
                    sp.wait_ge(h_lo, n + 1)
                    load_h(n + 1, h_in_sb, h_in)
                for q in range(TS):
                    sp.wait_ge(y_ready, 1 + n * TS + q + 1)
                    sp.dma_start(out_by_run[:, bass.ds(n * TS + q, 1), :].rearrange("p t d -> p (t d)"), y_out[q % 2][:, :])\
                        .then_inc(y_stored[q % 2], 16)

            ffn_tile(0, True, False)
            with sp.Fori(0, (NF - 2) // 2) as it:
                ffn_tile(it * 2 + 1, False, False)
                ffn_tile(it * 2 + 2, False, False)
            ffn_tile(NF - 1, False, True)
            for i in range(2):
                sp.wait_ge(y_stored[i], 16 + 16 * NF * TS // 2)

        @block.gpsimd
        def _(gp):
            nc.gpsimd.memset(ident[:, :], 0.0).then_inc(setup_gps, 1)
            nc.gpsimd.memset(own_mask[:, :], 1.0).then_inc(setup_gps, 1)
            nc.gpsimd.memset(prev_mask[:, :], 1.0).then_inc(setup_gps, 1)
            nc.gpsimd.memset(own_pred[:, :], 1).then_inc(setup_gps, 1)
            nc.gpsimd.memset(ones[:, :], 1.0).then_inc(setup_gps, 1)
            nc.gpsimd.memset(v_nat[:, 3, :], 0.0).then_inc(setup_gps, 1)
            gp.wait_ge(setup_gps, 6)
            nc.gpsimd.affine_select(out=ident[:, :], in_=ident[:, :], compare_op=ALU.not_equal, fill=1.0,
                                    base=0, pattern=[[-1, P]], channel_multiplier=1).then_inc(setup_gps, 1)
            nc.gpsimd.affine_select(out=own_mask[:, :], in_=own_mask[:, :], compare_op=ALU.is_ge, fill=0.0,
                                    base=0, pattern=[[1, P]], channel_multiplier=-1).then_inc(setup_gps, 1)
            nc.gpsimd.affine_select(out=prev_mask[:, :], in_=prev_mask[:, :], compare_op=ALU.is_ge, fill=0.0,
                                    base=-1, pattern=[[-1, P]], channel_multiplier=1).then_inc(setup_gps, 1)
            nc.gpsimd.affine_select(out=own_pred[:, :], in_=own_pred[:, :], compare_op=ALU.is_ge, fill=0,
                                    base=0, pattern=[[-1, P]], channel_multiplier=1).then_inc(setup_gps, 1)
            for t in kT:
                nc.gpsimd.memset(t[:, :, 3, :].bitcast(F32), 0.0).then_inc(setup_gps, 1)

            def tile(n, par, kind, half):
                for u in range(UNITS):
                    gp.wait_ge(inv_ready, n * UNITS + u + 1)
                    nc.gpsimd.tensor_tensor(probs[u % 4][:, :, :], probs[u % 4][:, :, :],
                                            row_inv[:, u % 4, :].unsqueeze(2).to_broadcast([P, GH, P]),
                                            ALU.mult).then_inc(norm_done, 1)

            all_tiles(gp, tile)

            emptied(gp, LAST, "xp1_")
            gp.wait_ge(res_out, 16 + 16 * NT)
            gp.wait_ge(xp_out, 16 + 16 * (NT - 2))
            gp.dma_start(b2_rows[:, :], b2.rearrange("(a n) -> a n", a=1).to_broadcast([P, D])).then_inc(b2_in, 16)
            for k in range(2):
                gp.dma_start(w1_stage[k][:, :], w1[k * P:(k + 1) * P, :]).then_inc(w1_in[k], 16)
            for m in range(FC):
                gp.dma_start(w2_stage[m][:, :], w2[m * P:(m + 1) * P, :]).then_inc(w2_in, 16)
            for k in range(DC):
                gp.wait_ge(w1_in[k % 2], 16 * (k // 2 + 1))
                nc.gpsimd.tensor_copy(w1_s[0][:, k, :], w1_stage[k % 2][:, :]).then_inc(w1_hi, 1)
                gp.wait_ge(w1_hi, k + 1)
                nc.gpsimd.tensor_tensor(w1_s[1][:, k, :], w1_stage[k % 2][:, :], w1_s[0][:, k, :].bitcast(F32),
                                        ALU.subtract).then_inc(w1_lo, 1)
                if k + 2 < DC:
                    gp.wait_ge(w1_lo, k + 1)
                    gp.dma_start(w1_stage[k % 2][:, :], w1[(k + 2) * P:(k + 3) * P, :]).then_inc(w1_in[k % 2], 16)
            for m in range(FC):
                gp.wait_ge(w2_hi, m + 1)
                nc.gpsimd.tensor_tensor(w2_s[1][:, m, :], w2_stage[m][:, :], w2_s[0][:, m, :].bitcast(F32),
                                        ALU.subtract).then_inc(w2_lo, 1)
            gp.wait_ge(b2_in, 16)
            with gp.Fori(0, NF) as n:
                gp.wait_ge(res_back, (n + 1) * 16)
                nc.gpsimd.tensor_tensor(res_in[:, :, :], res_in[:, :, :],
                                        b2_rows[:, :].unsqueeze(1).to_broadcast([P, TS, D]), ALU.add).then_inc(res_b2, 1)

        @block.scalar
        def _(act):
            for b in range(B):
                act.dma_start(cond_T[:, :, b], cond[b].rearrange("(c p) -> p c", p=P),
                              allow_slow_non_contiguous=True).then_inc(cond_in, 16)
            act.dma_start(bh_T[:, :], b_h.rearrange("(c p) -> p c", p=P), allow_slow_non_contiguous=True).then_inc(biases_in, 16)
            act.dma_start(b1_T[:, :], b1.rearrange("(c p) -> p c", p=P), allow_slow_non_contiguous=True).then_inc(biases_in, 16)
            act.nop().then_inc(exp_done, CREDIT)
            act.nop().then_inc(h_done, DC)
            act.nop().then_inc(relu_done, 4)

            def w_part(i):
                act.wait_ge(w_in[i], 16 * (GH if i == 4 else 1))
                nc.scalar.activation(parts[i][2][0], parts[i][0], ACT.Copy).then_inc(w_hi, 1)

            def full(plan, item):
                act.wait_ge(work_full, plan.first_use + item.use + 1)

            def emit(plan, item, n, par):
                name, w = item.kind, item.w
                if name == "oT":
                    act.wait_ge(pv_done, CREDIT + n * UNITS + (w + 1) * DC)
                    nc.scalar.activation(oT[0][:, :, :], o_bank, ACT.Copy).then_inc(split_hi, 1)
                    return
                if name == "out":
                    return
                full(plan, item)
                bank = work_bank[item.use % 2]
                if name == "xT":
                    for j in range(2):
                        last = nc.scalar.activation(xT[0][:, 2 * w + j, :], bank[:, j * TT:(j + 1) * TT], ACT.Copy,
                                                    scale=ys_now[:, 2 * w + j:2 * w + j + 1])
                    last.then_inc(split_hi, 1)
                elif name == "cT":
                    for j in range(2):
                        last = nc.scalar.activation(cT[0][:, 2 * w + j, :], bank[:, j * TT:(j + 1) * TT], ACT.Copy,
                                                    scale=demod_now[:, 2 * w + j:2 * w + j + 1])
                    last.then_inc(split_hi, 1)
                elif name == "x1T":
                    nc.scalar.activation(x1T[0][:, 2 * w:2 * w + 2, :], bank.rearrange("p (c t) -> p c t", c=2),
                                         ACT.Copy).then_inc(split_hi, 1)
                elif name == "q":
                    nc.scalar.activation(qT[0][:, 2 * w:2 * w + 2, :], bank.rearrange("p (c t) -> p c t", c=2),
                                         ACT.Copy).then_inc(split_hi, 1)
                elif name == "k":
                    nc.scalar.activation(kT[0][:, 2 * w:2 * w + 2, 2 * par:2 * par + 2, :],
                                         bank.rearrange("p (g s t) -> p g s t", g=2, s=2), ACT.Copy)\
                        .then_inc(split_hi, 1)
                elif name == "v":
                    nc.scalar.activation(v_nat[:, 2 * par + w, :], bank, ACT.Copy).then_inc(work_empty[item.use % 2], 1)
                elif name == "xp":
                    if w == 0 and not plan.last:
                        act.wait_ge(xp_out, 16 * n)
                    for j in range(2):
                        c = 2 * w + j
                        if plan.last:
                            k = NT - 1 if item.name[-1] == "_" else NT - 2
                            dst = xp[:, c, k * CPT:(k + 1) * CPT, :].rearrange("p n t -> p (n t)")
                        else:
                            dst = xp_stage[:, c, :]
                        last = nc.scalar.activation(dst, bank[:, j * TT:(j + 1) * TT], ACT.Identity,
                                                    bias=bh_T[:, c:c + 1])
                    last.then_inc(work_empty[item.use % 2], 1)

            act.wait_ge(now_set, 1)
            for i, row in enumerate(before.slots):
                if i == 1:
                    w_part(0)
                    w_part(1)
                    act.wait_ge(setup_dve, 3)
                    nc.scalar.activation(demod[:, :, :], ys[:, :, :], ACT.Sqrt).then_inc(setup_act, 1)
                    nc.scalar.activation(row_sum[:, 0:2, :].rearrange("p a b -> p (a b)"),
                                         ys[:, :, :].rearrange("p a b -> p (a b)"), ACT.Exp)
                    act.wait_ge(demod_set, 1)
                elif i > 1:
                    w_part(i)
                for item in row:
                    emit(before, item, 0, 0)
            act.wait_ge(biases_in, 32)
            act.wait_ge(setup_gps, SET_ALL)

            def tile(n, par, kind, half):
                plan = plan_of(n, kind)
                for s in range(len(plan.slots)):
                    row = plan.slots[s]
                    if kind != "last" and s == plan.items["xT0"].slot:
                        act.wait_ge(now_set, n + 2)
                    if row and row[0].name[:2] == "oT":
                        emit(plan, row[0], n, par)
                        row = row[1:]
                    soon = ("v1_",) if s == 0 and kind != "first" else \
                        tuple(item.name for item in row if item.kind in ("xT", "x1T", "xp"))
                    for item in row:
                        if item.name in soon:
                            emit(plan, item, n, par if item.name == "v1_" else 1 - par)
                    row = [item for item in row if item.name not in soon]
                    if s < UNITS:
                        U = n * UNITS + s
                        act.wait_ge(max_ready, U + 1)
                        act.wait_ge(turn_done, CREDIT + U + 1 - 4)
                        for r in range(GH):
                            last = nc.scalar.activation(
                                probs[s % 4][:, r, :], scores_of(par, s)[1][:, r, :], ACT.Exp,
                                bias=neg_max[:, s % 4, r:r + 1], scale=SCALE, accum_out=row_sum[:, s % 4, r:r + 1])
                        last.then_inc(exp_done, 1)
                    if kind == "first" and s == 1:
                        w_part(WEIGHTS - 1)
                    for item in row:
                        emit(plan, item, n, 1 - par)

            all_tiles(act, tile)

            act.wait_ge(flag_ready, 1)
            sweep, again = act.alloc_register("act_sweep"), act.alloc_register("act_again")
            act.reg_mov(sweep, 0)
            act.reg_mov(again, 1)
            with act.While(lambda: act.snap(again)):
                s = act.snap(sweep, min_val=0, max_val=MAX_SWEEPS)

                def step(tr, j):
                    act.wait_ge(h_out[j], 16 + (s * (RUN // HR) + tr) * 16)
                    for m in range(DC):
                        act.wait_ge(add_done, (s * RUN + tr * HR + j) * DC + m + 1)
                        nc.scalar.activation(states[:, j, m, :], pre[:, j % 2, m, :], ACT.Tanh).then_inc(h_done, 1)

                with act.Fori(0, RUN // HR - 1) as tr:
                    for j in range(HR):
                        step(tr, j)
                for j in range(HR):
                    act.wait_ge(h_early, (s + 1) * 16)
                    nc.scalar.activation(h_s[0][0][:, j, :, :], h_first[:, j, :, :], ACT.Copy).then_inc(h_first_hi, 1)
                    step(RUN // HR - 1, j)
                act.wait_ge(flag_ready, s + 2)
                act.reg_add(sweep, sweep, 1)
                act.reg_load(again, sweep_on[0:1, 0:1])

            act.wait_ge(scan_over, 1)

            def h_part(n, par):
                act.wait_ge(h_in, n * 16)
                nc.scalar.activation(h_s[par][0][:, :, :, :].rearrange("p t c n -> p (t c n)"),
                                     h_in_sb[:, :, :, :].rearrange("p t c n -> p (t c n)"), ACT.Copy).then_inc(h_hi, 1)

            def ffn_tile(n, par, first, last):
                for m in range(FC):
                    if first and m < FC // 2:
                        if m == 0:
                            act.wait_ge(w2_in, 16 * FC)
                        for c in (2 * m, 2 * m + 1):
                            nc.scalar.activation(w2_s[0][:, c, :], w2_stage[c][:, :], ACT.Copy).then_inc(w2_hi, 1)
                    act.wait_ge(hid_full, n * FC + m + 1)
                    act.wait_ge(hid_split, 2 + n * FC + m - 1)
                    nc.scalar.activation(hid_tmp[m % 2][:, :], ps[:, m % 4, :], ACT.Relu, bias=b1_T[:, m:m + 1])\
                        .then_inc(relu_done, 1)
                    if m == H_AT and not last:
                        if first:
                            act.wait_ge(w2_lo, FC)
                        h_part(n + 1, 1 - par)

            ffn_tile(0, 0, True, False)
            with act.Fori(0, (NF - 2) // 2) as it:
                ffn_tile(it * 2 + 1, 1, False, False)
                ffn_tile(it * 2 + 2, 0, False, False)
            ffn_tile(NF - 1, 1, False, True)

        @block.vector
        def _(dve):
            step = [0]

            def then(ins):
                step[0] += 1
                ins.then_inc(setup_dve, 1)
                dve.wait_ge(setup_dve, step[0])

            dve.sem_inc(masked, 1)
            dve.sem_inc(o_ready, 1)
            dve.sem_inc(y_ready, 1)
            dve.sem_inc(hid_split, 2)
            def w_rest(i):
                dve.wait_ge(w_hi, i + 1)
                nc.vector.tensor_tensor(parts[i][2][1], parts[i][0], parts[i][2][0].bitcast(F32),
                                        ALU.subtract).then_inc(w_lo, 1)

            def lo_part(plan, item, n, par):
                name, w = item.kind, item.w
                if name == "out":
                    dve.wait_ge(work_full, plan.first_use + item.use + 1)
                    if w == 0:
                        dve.wait_ge(res_out, 16 + n * 16)
                    nc.vector.tensor_tensor(x1_nat[:, w, :], work_bank[item.use % 2], x_nat[par][:, w, :], ALU.add)\
                        .then_inc(work_empty[item.use % 2], 1)
                    return
                if item.split is None:
                    return
                dve.wait_ge(split_hi, plan.first_split + item.split + 1)
                if name == "oT":
                    nc.vector.tensor_tensor(oT[1][:, :, :], o_bank, oT[0][:, :, :].bitcast(F32), ALU.subtract)\
                        .then_inc(o_ready, 1)
                    return
                bank = work_bank[item.use % 2]
                if name == "x1T":
                    last = nc.vector.tensor_tensor(x1T[1][:, 2 * w:2 * w + 2, :], bank.rearrange("p (c t) -> p c t", c=2),
                                                   x1T[0][:, 2 * w:2 * w + 2, :].bitcast(F32), ALU.subtract)
                elif name == "q":
                    last = nc.vector.tensor_tensor(qT[1][:, 2 * w:2 * w + 2, :], bank.rearrange("p (c t) -> p c t", c=2),
                                                   qT[0][:, 2 * w:2 * w + 2, :].bitcast(F32), ALU.subtract)
                elif name == "k":
                    last = nc.vector.tensor_tensor(kT[1][:, 2 * w:2 * w + 2, 2 * par:2 * par + 2, :],
                                                   bank.rearrange("p (g s t) -> p g s t", g=2, s=2),
                                                   kT[0][:, 2 * w:2 * w + 2, 2 * par:2 * par + 2, :].bitcast(F32),
                                                   ALU.subtract)
                else:
                    dst, factor = (xT, ys_now) if name == "xT" else (cT, demod_now)
                    for j in range(2):
                        c = 2 * w + j
                        last = nc.vector.scalar_tensor_tensor(
                            out=dst[1][:, c, :], in0=bank[:, j * TT:(j + 1) * TT], scalar=factor[:, c:c + 1],
                            in1=dst[0][:, c, :].bitcast(F32), op0=ALU.mult, op1=ALU.subtract)
                last.then_inc(work_empty[item.use % 2], 1)

            dve.wait_ge(cond_in, 16 * B)
            then(nc.vector.tensor_scalar(ys[:, :, :], cond_T[:, :, :], COND_SCALE, None, ALU.mult))
            nc.vector.tensor_copy(ys_now[:, :], ys[:, :, 0]).then_inc(now_set, 1)
            for b in range(B):
                nc.vector.tensor_copy(ys_tile[:, b * TPB:(b + 1) * TPB, :],
                                      ys[:, :, b].unsqueeze(1).to_broadcast([P, TPB, DC]))
            nc.vector.memset(before_tile[:, :], 0.0)
            dve.wait_ge(now_set, 1)
            for item in before.slots[0]:
                lo_part(before, item, 0, 0)
            dve.wait_ge(w_in[0], 16)
            for i, sq in enumerate(w_sq):
                half = stage_probs[:, 2 * i:2 * i + 2, :].rearrange("p a b -> p (a b)")
                nc.vector.tensor_tensor(sq[:, :, :].rearrange("p a b -> p (a b)"), half, half, ALU.mult)
            then(nc.vector.tensor_tensor(ys_sq[:, :, :], ys[:, :, :], ys[:, :, :], ALU.mult))
            for b in range(B):
                i = b * TPB // 2
                nc.vector.memset(before_tile[:, i:i + 1], NEG_INF)
            w_rest(0)
            dve.wait_ge(setup_pe, 1)
            then(nc.vector.tensor_scalar(ys[:, :, :], ps[:, 2, 0:DC * B].rearrange("p (c b) -> p c b", b=B),
                                         EPS, None, ALU.add))
            dve.wait_ge(setup_act, 1)
            then(nc.vector.reciprocal(demod[:, :, :], demod[:, :, :]))
            nc.vector.tensor_copy(demod_now[:, :], demod[:, :, 0]).then_inc(demod_set, 1)
            for b in range(B):
                nc.vector.tensor_copy(demod_tile[:, b * TPB:(b + 1) * TPB, :],
                                      demod[:, :, b].unsqueeze(1).to_broadcast([P, TPB, DC]))
            w_rest(1)
            dve.wait_ge(demod_set, 1)
            for i, row in enumerate(before.slots):
                if i > 1:
                    w_rest(i)
                for item in row if i > 0 else []:
                    lo_part(before, item, 0, 0)
            dve.wait_ge(setup_gps, SET_ALL)

            def tile(n, par, kind, half):
                plan = plan_of(n, kind)
                count = [0]

                def own(ins):
                    count[0] += 1
                    ins.then_inc(dve_step, 1)
                    dve.wait_ge(dve_step, steps_before(n, half) + count[0])

                if par == 0:
                    own(nc.vector.tensor_copy(before_now[:, :], before_tile[:, bass.ds(half, 1)]))

                def max_of(u):
                    dve.wait_ge(scores_done, n * UNITS + u + 1)
                    _, prev, own_s = scores_of(par, u)
                    if par == 0 and u < DC:
                        own(nc.vector.tensor_scalar(prev, prev, before_now[:, 0:1], None, ALU.add))
                    dve.sem_inc(select_gate, 1)
                    own(nc.vector.copy_predicated(prev, own_pred[:, :].unsqueeze(1).to_broadcast([P, GH, P]), own_s))
                    own(nc.vector.reduce_max(row_max[:, u % 4, :], prev, AX_X))
                    nc.vector.tensor_scalar(neg_max[:, u % 4, :], row_max[:, u % 4, :], -SCALE, None, ALU.mult)\
                        .then_inc(max_ready, 1)

                def invert(u):
                    dve.wait_ge(exp_done, CREDIT + n * UNITS + u + 1)
                    nc.vector.reciprocal(row_inv[:, u % 4, :], row_sum[:, u % 4, :]).then_inc(inv_ready, 1)

                def mask(u):
                    dve.wait_ge(turn_done, CREDIT + n * UNITS + u + 1)
                    dve.wait_ge(pv_done, CREDIT + n * UNITS + u - 1)
                    nc.vector.tensor_tensor(own_T[u % 2][:, :, :], turn_bank,
                                            own_mask[:, :].unsqueeze(1).to_broadcast([P, GH, P]), ALU.mult)
                    nc.vector.tensor_tensor(prev_T[u % 2][:, :, :], turn_bank,
                                            prev_mask[:, :].unsqueeze(1).to_broadcast([P, GH, P]), ALU.mult)\
                        .then_inc(masked, 1)

                for s in range(len(plan.slots)):
                    row = plan.slots[s]
                    if kind != "last" and s == plan.items["xT0"].slot:
                        nc.vector.tensor_copy(ys_now[:, :], ys_tile[:, bass.ds(n + 1, 1), :].rearrange("p b c -> p (b c)"))
                        nc.vector.tensor_copy(demod_now[:, :], demod_tile[:, bass.ds(n + 1, 1), :].rearrange("p b c -> p (b c)"))\
                            .then_inc(now_set, 1)
                        dve.wait_ge(now_set, n + 2)
                    if s < UNITS:
                        max_of(s)
                    for item in row:
                        if item.kind in TURNS:
                            lo_part(plan, item, n, 1 - par)
                    if 0 <= s - 1 < UNITS:
                        invert(s - 1)
                    if kind == "first" and s == 2:
                        w_rest(WEIGHTS - 1)
                    if 0 <= s - LAG_T < UNITS:
                        mask(s - LAG_T)
                    for item in row:
                        if item.kind not in TURNS:
                            lo_part(plan, item, n, par if item.kind == "out" else 1 - par)

            all_tiles(dve, tile)

            dve.wait_ge(work_full, LAST.first_use + LAST.items["x1T1_"].use + 1)
            dve.wait_ge(res_out, 16 + 16 * NT)
            then(nc.vector.memset(starts[:, :, :], 0.0))
            for b in range(B):
                last = nc.vector.tensor_copy(starts[:, :, b * CPB:b * CPB + 1], cond_T[:, :, b:b + 1])
            last.then_inc(flag_ready, 1)
            dve.wait_ge(xp_in, 16 * (NT - 2))

            sweep, again = dve.alloc_register("dve_sweep"), dve.alloc_register("dve_again")
            dve.reg_mov(sweep, 0)
            dve.reg_mov(again, 1)
            with dve.While(lambda: dve.snap(again)):
                s = dve.snap(sweep, min_val=0, max_val=MAX_SWEEPS)

                def step(tr, j):
                    for m in range(DC):
                        dve.wait_ge(mm_done, (s * RUN + tr * HR + j) * DC + m + 1)
                        nc.vector.tensor_tensor(
                            pre[:, j % 2, m, :], ps[:, (j % 2) * DC + m, 0:COLS],
                            xp[:, m, :, bass.ds(tr * HR + j, 1)].rearrange("p n t -> p (n t)"),
                            ALU.add).then_inc(add_done, 1)

                def first_rest(j):
                    dve.wait_ge(h_first_hi, s * TS + j + 1)
                    nc.vector.tensor_tensor(h_s[0][1][:, j, :, :], h_first[:, j, :, :],
                                            h_s[0][0][:, j, :, :].bitcast(F32), ALU.subtract)

                with dve.Fori(0, RUN // HR - 1) as tr:
                    for j in range(HR):
                        step(tr, j)
                for j in range(HR):
                    step(RUN // HR - 1, j)
                    first_rest(j)
                STEPS = B + 4
                ends = states[:, HR - 1, :, :]
                dve.wait_ge(h_done, DC + (s + 1) * RUN * DC)
                for b in range(B):
                    lo = b * CPB
                    nc.vector.tensor_tensor(drift[:, :, lo:lo + CPB - 1], ends[:, :, lo:lo + CPB - 1],
                                            starts[:, :, lo + 1:lo + CPB], ALU.subtract).then_inc(state_step, 1)
                dve.wait_ge(state_step, s * STEPS + B)
                by_b = drift[:, :, :].rearrange("p c (b n) -> p c b n", b=B)[:, :, :, 0:CPB - 1]
                nc.vector.tensor_tensor(by_b, by_b, by_b, ALU.mult).then_inc(state_step, 1)
                dve.wait_ge(state_step, s * STEPS + B + 1)
                nc.vector.tensor_reduce(worst[:, :], by_b, mybir.AxisListType.XYZ, ALU.max).then_inc(state_step, 1)
                dve.wait_ge(state_step, s * STEPS + B + 2)
                nc.vector.tensor_scalar(off[:, :], worst[:, :], STATE_TOLERANCE ** 2, None, ALU.is_gt)\
                    .then_inc(off_ready, 1)
                for b in range(B):
                    lo = b * CPB
                    last = nc.vector.tensor_copy(starts[:, :, lo + 1:lo + CPB], ends[:, :, lo:lo + CPB - 1])
                last.then_inc(state_step, 1)
                dve.wait_ge(state_step, s * STEPS + B + 3)
                dve.wait_ge(count_ready, s + 1)
                nc.vector.tensor_copy(sweep_on[0:1, 0:1], ps[0:1, 0, 0:1]).then_inc(flag_ready, 1)
                dve.nop().then_inc(state_step, 1)
                dve.wait_ge(flag_ready, s + 2)
                dve.reg_add(sweep, sweep, 1)
                dve.reg_load(again, sweep_on[0:1, 0:1])
            dve.nop().then_inc(scan_over, 1)
            dve.nop().then_inc(h_lo, 1)

            def h_rest(n, par):
                dve.wait_ge(h_hi, n)
                nc.vector.tensor_tensor(h_s[par][1][:, :, :, :].rearrange("p t c n -> p (t c n)"),
                                        h_in_sb[:, :, :, :].rearrange("p t c n -> p (t c n)"),
                                        h_s[par][0][:, :, :, :].rearrange("p t c n -> p (t c n)").bitcast(F32),
                                        ALU.subtract).then_inc(h_lo, 1)

            def ffn_tile(n, par, last):
                for m in range(FC):
                    dve.wait_ge(relu_done, 4 + n * FC + m + 1)
                    dve.wait_ge(hid_used, 4 + n * FC + m - 3)
                    nc.vector.tensor_copy(hid_s[m % 4][0][:, :], hid_tmp[m % 2][:, :]).then_inc(hid_hi, 1)
                    dve.wait_ge(hid_hi, n * FC + m + 1)
                    nc.vector.tensor_tensor(hid_s[m % 4][1][:, :], hid_tmp[m % 2][:, :], hid_s[m % 4][0][:, :].bitcast(F32),
                                            ALU.subtract).then_inc(hid_split, 1)
                    if m == H_AT and not last:
                        h_rest(n + 1, 1 - par)
                for q in range(TS):
                    dve.wait_ge(y_full, n * TS + q + 1)
                    dve.wait_ge(res_b2, n + 1)
                    dve.wait_ge(y_stored[q % 2], 16 + (n * (TS // 2) + q // 2) * 16)
                    nc.vector.tensor_tensor(y_out[q % 2][:, :], ps[:, 4 + q, :], res_in[:, q, :], ALU.add)\
                        .then_inc(y_ready, 1)

            ffn_tile(0, 0, False)
            with dve.Fori(0, (NF - 2) // 2) as it:
                ffn_tile(it * 2 + 1, 1, False)
                ffn_tile(it * 2 + 2, 0, False)
            ffn_tile(NF - 1, 1, True)

        @block.tensor
        def _(pe):
            for j in range(2):
                pe.nop().then_inc(work_empty[j], 1)
            pe.nop().then_inc(turn_done, CREDIT)
            pe.nop().then_inc(pv_done, CREDIT)
            pe.nop().then_inc(hid_used, 4)
            def three(dst, a, b, first, last, at=(0, 0)):
                nc.tensor.matmul(dst, a[0], b[0], start=first, stop=False, tile_position=at)
                nc.tensor.matmul(dst, a[0], b[1], start=False, stop=False, tile_position=at)
                return nc.tensor.matmul(dst, a[1], b[0], start=False, stop=last, tile_position=at)

            def turn(bank, src, w):
                for j in range(2):
                    for q in range(BLK):
                        c = 2 * w + j
                        last = nc.tensor.transpose(bank[:, j * TT + q * P:j * TT + (q + 1) * P],
                                                   src[:, q, c * P:(c + 1) * P], ident[:, :])
                return last

            def product(bank, weight, col, src, w, chunks=(0, 1)):
                for j in chunks:
                    c = col + (2 * w + j) * P
                    for k in range(DC):
                        last = three(bank[:, j * TT:(j + 1) * TT], [p[:, k, c:c + P] for p in weight],
                                     [p[:, k, :] for p in src], k == 0, k == DC - 1)
                return last

            def rows(bank, src, q, weight, col):
                for k in range(DC):
                    last = three(bank, [p[:, k, q * P:(q + 1) * P] for p in src],
                                 [p[:, k, col:col + D] for p in weight], k == 0, k == DC - 1)
                return last

            def emit(plan, item, par, half, chunks=(0, 1)):
                name, w, bank = item.kind, item.w, work_bank[item.use % 2]
                if 0 in chunks:
                    pe.wait_ge(work_empty[item.use % 2], 1 + plan.rounds + item.use // 2)
                if name == "xT":
                    if w == 0:
                        pe.wait_ge(x_in[par], 16 * (half + 1))
                    last = turn(bank, x_nat[par], w)
                elif name == "cT":
                    if w == 0:
                        emptied(pe, plan, "xT1")
                    last = product(bank, w_cond_s, 0, xT, w)
                elif name == "q":
                    last = product(bank, w_qkv_s, 0, cT, w, chunks)
                elif name == "k":
                    if w == 0:
                        emptied(pe, plan, "cT1")
                    last = product(bank, w_qkv_s, D, cT, w)
                elif name == "v":
                    last = rows(bank, cT, w, w_qkv_s, 2 * D)
                elif name == "out":
                    last = rows(bank, oT, 0, w_out_s, 0)
                elif name == "x1T":
                    if w == 0 and item.name == "x1T0_":
                        emptied(pe, plan, "out1")
                    elif w == 0:
                        last_emptied(pe, plan)
                    last = turn(bank, x1_nat, w)
                elif name == "xp":
                    if w == 0:
                        emptied(pe, plan, item.name.replace("xp0", "x1T1"))
                    last = product(bank, w_x_s, 0, x1T, w)
                if 1 in chunks:
                    last.then_inc(work_full, 1)

            pe.wait_ge(setup_gps, SET_IDENT)
            for row in before.slots:
                for item in row:
                    if item.name == "cT0":
                        pe.wait_ge(setup_dve, 2)
                        for m in range(DC):
                            for k in range(DC):
                                sq = w_sq[k // 2][:, :, :].rearrange("p a b -> p (a b)")
                                at = (k % 2) * D + m * P
                                last = nc.tensor.matmul(ps[:, 2, m * B:(m + 1) * B], sq[:, at:at + P],
                                                        ys_sq[:, k, :], start=(k == 0), stop=(k == DC - 1))
                        last.then_inc(setup_pe, 1)
                        pe.wait_ge(w_lo, 1)
                    if item.name in ("k0", "q0", "v0"):
                        pe.wait_ge(w_lo, 2 + ("k0", "q0", "v0").index(item.name))
                    emit(before, item, 0, 0)
            pe.wait_ge(setup_dve, 3)

            def tile(n, par, kind, half):
                plan = plan_of(n, kind)

                def scores(u):
                    q, g = divmod(u, DC)
                    slot = 2 * par + q
                    if u == 0 and kind == "first":
                        pe.wait_ge(setup_gps, SET_ALL)
                    pe.wait_ge(exp_done, CREDIT + n * UNITS + u - 1)
                    both = slice(0, 4, 3) if slot == 0 else slice(slot - 1, slot + 1)
                    rows = slice(g * HEAD, (g + 1) * HEAD)
                    for r in range(GH):
                        last = three(scores_of(par, u)[0][:, r, :].rearrange("p (s k) -> p s k", s=2),
                                     [t[rows, r, q * P:(q + 1) * P] for t in qT], [t[rows, r, both, :] for t in kT],
                                     True, True, (g * HEAD, 0))
                    last.then_inc(scores_done, 1)

                def turn_probs(u):
                    pe.wait_ge(norm_done, n * UNITS + u + 1)
                    pe.wait_ge(masked, 1 + n * UNITS + u)
                    for r in range(GH):
                        last = nc.tensor.transpose(turn_bank[:, r, :], probs[u % 4][:, r, :], ident[:, :])
                    last.then_inc(turn_done, 1)

                def probs_v(u):
                    q, g = divmod(u, DC)
                    slot = 2 * par + q
                    if u == 0 and kind == "first":
                        last_emptied(pe, plan)
                    elif u == 0:
                        emptied(pe, plan, "v1_")
                    pe.wait_ge(masked, 1 + n * UNITS + u + 1)
                    if g == 0:
                        pe.wait_ge(o_ready, 1 + n * BLK + q)
                    for probs_T, s, first in ((prev_T, (slot - 1) % 4, True), (own_T, slot, False)):
                        for r in range(GH):
                            cols = slice(r * P + g * HEAD, r * P + (g + 1) * HEAD)
                            last = nc.tensor.matmul(o_bank[r * HEAD:(r + 1) * HEAD, g, :], v_nat[:, s, cols],
                                                    probs_T[u % 2][:, r, :], start=first, stop=not first,
                                                    tile_position=(0, r * HEAD))
                    last.then_inc(pv_done, 1)

                for s, row in enumerate(plan.slots):
                    if s < UNITS:
                        scores(s)
                    if 0 <= s - LAG_T < UNITS:
                        turn_probs(s - LAG_T)
                    if 0 <= s - LAG_V < UNITS:
                        probs_v(s - LAG_V)
                    for item in row:
                        if item.kind == "oT":
                            continue
                        if item.kind == "out":
                            pe.wait_ge(o_ready, 1 + n * BLK + item.w + 1)
                            if kind == "first":
                                pe.wait_ge(w_lo, WEIGHTS)
                        emit(plan, item, 1 - par, half, (1,) if item.name in HALF_AHEAD else (0, 1))
                    for item in sum(plan.slots[s + 1:s + 2], []):
                        if item.name in HALF_AHEAD:
                            emit(plan, item, 1 - par, half, (0,))

            all_tiles(pe, tile)

            emptied(pe, LAST, "xp0_")
            emptied(pe, LAST, "xp1_")
            pe.wait_ge(w_h_in, 16)
            pe.wait_ge(flag_ready, 1)
            sweep, again = pe.alloc_register("pe_sweep"), pe.alloc_register("pe_again")
            pe.reg_mov(sweep, 0)
            pe.reg_mov(again, 1)
            order = [(m, k) for m in (0, 1) for k in range(DC - 1)] + [(0, DC - 1), (1, DC - 1)] + \
                    [(m, k) for m in range(2, DC) for k in range(DC)]
            with pe.While(lambda: pe.snap(again)):
                s = pe.snap(sweep, min_val=0, max_val=MAX_SWEEPS)

                def step(tr, j, last_states):
                    G = s * RUN + tr * HR + j
                    waited = 0
                    for m, k in order:
                        if k >= waited:
                            pe.wait_ge(h_done, G * DC + k + 1)
                            waited = k + 1
                        ins = nc.tensor.matmul(ps[:, (j % 2) * DC + m, 0:COLS], w_h_sb[:, k, m * P:(m + 1) * P],
                                               last_states[:, k, :], start=(k == 0), stop=(k == DC - 1))
                        if k == DC - 1:
                            ins.then_inc(mm_done, 1)

                for j in range(HR):
                    step(0, j, states[:, j - 1, :, :] if j > 0 else starts)
                with pe.Fori(1, RUN // HR) as tr:
                    for j in range(HR):
                        step(tr, j, states[:, (j - 1) % HR, :, :])
                pe.wait_ge(off_ready, s + 1)
                nc.tensor.matmul(ps[0:1, 0, 0:1], off[:, :], ones[:, :], start=True, stop=True).then_inc(count_ready, 1)
                pe.wait_ge(flag_ready, s + 2)
                pe.reg_add(sweep, sweep, 1)
                pe.reg_load(again, sweep_on[0:1, 0:1])

            pe.wait_ge(w1_lo, DC)

            def ffn_tile(n, par, first):
                for i in range(FC + FL):
                    if i < FC:
                        m = i
                        if m == 0:
                            pe.wait_ge(h_lo, n + 1)
                        pe.wait_ge(relu_done, n * FC + m + 1)
                        for k in range(DC):
                            ins = three(ps[:, m % 4, :].rearrange("p (t n) -> p t n", t=TS),
                                        [p[:, k, m * P:(m + 1) * P] for p in w1_s],
                                        [p[:, :, k, :] for p in h_s[par]], k == 0, k == DC - 1)
                        ins.then_inc(hid_full, 1)
                    if i >= FL:
                        m = i - FL
                        if m == 0:
                            pe.wait_ge(y_ready, 1 + n * TS)
                        if first:
                            pe.wait_ge(w2_lo, m + 1)
                        pe.wait_ge(hid_split, 2 + n * FC + m + 1)
                        for q in range(TS):
                            ins = three(ps[:, 4 + q, :], [p[:, q * P:(q + 1) * P] for p in hid_s[m % 4]],
                                        [p[:, m, :] for p in w2_s], m == 0, m == FC - 1)
                            if m == FC - 1:
                                ins.then_inc(y_full, 1)
                        if m < FC - 1:
                            ins.then_inc(hid_used, 1)
                        else:
                            pe.nop().then_inc(hid_used, 1)

            ffn_tile(0, 0, True)
            with pe.Fori(0, (NF - 2) // 2) as it:
                ffn_tile(it * 2 + 1, 1, False)
                ffn_tile(it * 2 + 2, 0, False)
            ffn_tile(NF - 1, 1, False)


_INS = ["x", "cond_1024", "L0_cond_weight", "L0_attn_w_qkv", "L0_attn_w_out", "L0_cond2_Wx", "L0_cond2_Wh",
        "L0_cond2_b", "L0_ffn_W1", "L0_ffn_b1", "L0_ffn_W2", "L0_ffn_b2"]


def kernel(**inputs):
    import numpy as _np
    import concourse.bacc as _bacc
    from concourse import mybir as _mybir
    from concourse.bass_utils import run_bass_kernel_spmd as _run

    nc = _bacc.Bacc("TRN2", target_bir_lowering=False, num_devices=1)
    arrays, args = {}, []
    for name in _INS:
        a = _np.ascontiguousarray(inputs[name])
        arrays[f"in_{name}_dram"] = a
        args.append(nc.dram_tensor(f"in_{name}_dram", a.shape, _mybir.dt.from_np(a.dtype), kind="ExternalInput").ap())
    out = nc.dram_tensor("out_dram", inputs["x"].shape, _mybir.dt.float32, kind="ExternalOutput").ap()
    block_kernel(nc, *args, out)
    r = _run(nc, [arrays], core_ids=[0])
    return r.results[0]["out_dram"]
```
